# Optimizing a Trainium2 kernel written in Bass

```python
import numpy as np
import jax
import jax.numpy as jnp

def _softmax(x, axis=-1):
    return jax.nn.softmax(x, axis=axis)

def _gelu(x):
    return jax.nn.gelu(x, approximate=True)

def _silu(x):
    return jax.nn.silu(x)

def _sigmoid(x):
    return jax.nn.sigmoid(x)

def _layernorm(x, axis=-1, eps=1e-05):
    m = jnp.mean(x, axis=axis, keepdims=True)
    v = jnp.var(x, axis=axis, keepdims=True)
    return (x - m) / jnp.sqrt(v + eps)

def _scatter_add(tgt, idx, src, axis=0):
    return tgt.at[idx].add(src)

def _segment_sum(src, seg, n):
    return jax.ops.segment_sum(src, seg, n)
kernel_name = 'mk_adj_ffn_d1_adj_r2_a2bb0b'

def setup_inputs(seed: int=0):
    np.random.seed(seed)
    _w = jnp.asarray

    def _rec_inputs():
        import jax
        import jax.numpy as jnp
        _gk = jax.random.key(seed)
        x = -0.0002928 + 1 * jax.random.normal(jax.random.fold_in(_gk, 1), (2048, 256), jnp.float32)
        _w = (1.0 + jnp.arange(2048, dtype=jnp.float32)) ** (-0.5)
        _w = _w / _w.mean()
        _pij = jnp.clip(0.00195312 * _w[:, None] * _w[None, :], 0.0, 1.0)
        _a = jax.random.uniform(jax.random.fold_in(_gk, 2), (2048, 2048)) < _pij
        _a = jnp.logical_or(_a, jnp.eye(2048, dtype=bool))
        _af = _a.astype(jnp.float32)
        _af = _af * jax.random.uniform(jax.random.fold_in(_gk, 3), (2048, 2048), jnp.float32, 0.05, 1)
        adj = _af
        return (x, adj)
    x, adj = _rec_inputs()

    def _L0_gnn_setup():
        import jax, jax.numpy as jnp
        import numpy as np
        N = 4096
        DIN = 256
        DOUT = 256
        key = jax.random.key(seed)
        k1, k2, k3 = jax.random.split(key, 3)
        x = jax.random.normal(k1, (N, DIN), dtype=jnp.float32)
        adj = jax.random.uniform(k2, (N, N), dtype=jnp.float32)
        W = jax.random.normal(k3, (DIN, DOUT), dtype=jnp.float32) * (1.0 / np.sqrt(DIN))
        b = jnp.zeros((DOUT,), dtype=jnp.float32)
        return {'x': x, 'adj': adj, 'W': W, 'b': b}
    _L0_gnn_all = _L0_gnn_setup()
    _L0_gnn_in = {k: v for k, v in _L0_gnn_all.items() if k in ('W', 'b')}
    del _L0_gnn_all

    def _L0_ffn_setup():
        import jax, jax.numpy as jnp
        import numpy as np
        TOP_K = 2
        key = jax.random.key(seed)
        ks = jax.random.split(key, 4)
        B, S, D, H, E = (2, 2048, 256, 1024, 8)
        scale_in = 1.0 / np.sqrt(D)
        scale_h = 1.0 / np.sqrt(H)
        return {'x': jax.random.normal(ks[0], (B, S, D), dtype=jnp.float32), 'gate_w': jax.random.normal(ks[1], (D, E), dtype=jnp.float32) * scale_in, 'gate_b': jnp.zeros((E,), dtype=jnp.float32), 'w1': jax.random.normal(ks[2], (E, D, H), dtype=jnp.float32) * scale_in, 'b1': jnp.zeros((E, H), dtype=jnp.float32), 'w2': jax.random.normal(ks[3], (E, H, D), dtype=jnp.float32) * scale_h, 'b2': jnp.zeros((E, D), dtype=jnp.float32)}
    _L0_ffn_all = _L0_ffn_setup()
    _L0_ffn_in = {k: v for k, v in _L0_ffn_all.items() if k in ('gate_w', 'gate_b', 'w1', 'b1', 'w2', 'b2')}
    del _L0_ffn_all
    return {'x': x, 'adj': adj, 'L0_gnn_W': _L0_gnn_in['W'], 'L0_gnn_b': _L0_gnn_in['b'], 'L0_ffn_gate_w': _L0_ffn_in['gate_w'], 'L0_ffn_gate_b': _L0_ffn_in['gate_b'], 'L0_ffn_w1': _L0_ffn_in['w1'], 'L0_ffn_b1': _L0_ffn_in['b1'], 'L0_ffn_w2': _L0_ffn_in['w2'], 'L0_ffn_b2': _L0_ffn_in['b2']}

def reference(x, adj, L0_gnn_W, L0_gnn_b, L0_ffn_gate_w, L0_ffn_gate_b, L0_ffn_w1, L0_ffn_b1, L0_ffn_w2, L0_ffn_b2):
    import jax
    import jax.numpy as jnp

    def _L0_gnn_ref(x, adj, W, b):
        import jax, jax.numpy as jnp
        import numpy as np
        N = 4096
        DIN = 256
        DOUT = 256
        rowsum = adj.sum(axis=1)
        d_inv_sqrt = jnp.where(rowsum > 0, rowsum ** (-0.5), 0.0)
        normalized_adj = d_inv_sqrt[:, None] * adj * d_inv_sqrt[None, :]
        support = normalized_adj @ x
        out = support @ W + b
        return jax.nn.relu(out)

    def _L0_ffn_ref(x, gate_w, gate_b, w1, b1, w2, b2):
        import jax, jax.numpy as jnp
        import numpy as np
        TOP_K = 2
        B, S, D = x.shape
        E = gate_w.shape[1]
        flat_x = x.reshape(-1, D)
        gate_logits = flat_x @ gate_w + gate_b
        raw_weights = jax.nn.softmax(gate_logits, axis=-1)
        top_w, top_idx = jax.lax.top_k(raw_weights, TOP_K)
        one_hot = jax.nn.one_hot(top_idx, E, dtype=flat_x.dtype)
        gate_output = (one_hot * top_w[..., None]).sum(axis=-2)
        h = jax.nn.gelu(jnp.einsum('td,edh->teh', flat_x, w1) + b1, approximate=False)
        expert_out = jnp.einsum('teh,ehd->ted', h, w2) + b2
        combined = jnp.einsum('ted,te->td', expert_out, gate_output)
        return combined.reshape(B, S, -1)
    x = x + _L0_gnn_ref(_layernorm(x, axis=-1), adj, L0_gnn_W, L0_gnn_b)
    x = x + _L0_ffn_ref(_layernorm(x, axis=-1)[None], L0_ffn_gate_w, L0_ffn_gate_b, L0_ffn_w1, L0_ffn_b1, L0_ffn_w2, L0_ffn_b2)[0]
    return x

_drawn_inputs = setup_inputs


def setup_inputs(seed=0):
    import zlib

    import numpy as np

    out = dict(_drawn_inputs(seed))
    spreads = {'L0_gnn_b': (0.0, 0.1),
     'L0_ffn_gate_b': (0.0, 0.1),
     'L0_ffn_b1': (0.0, 0.296),
     'L0_ffn_b2': (0.0, 0.1)}
    factors = {}
    for name, (base, spread) in spreads.items():
        noise = np.random.default_rng([zlib.crc32(name.encode()), seed]).standard_normal(out[name].shape)
        drawn = base * np.exp(spread * noise) if base else spread * noise
        out[name] = jnp.asarray(drawn.astype(out[name].dtype))
    for name, factor in factors.items():
        out[name] = (out[name] * factor).astype(out[name].dtype)
    return out
```

```python
from contextlib import ExitStack

import concourse.bass as bass
from concourse import mybir

F32, F16, BF16 = mybir.dt.float32, mybir.dt.float16, mybir.dt.bfloat16
I32, U32 = mybir.dt.int32, mybir.dt.uint32
ACT, ALU, AX = mybir.ActivationFunctionType, mybir.AluOpType, mybir.AxisListType

P = 128
N, D, H, E, TOPK = 2048, 256, 1024, 8, 2
T = N // P
KD = D // P
HT = H // P
NT = TOPK * T + E - 1
REGION = N + P
EMPTY = E * REGION
ROW = D + E + 1
GATE0, IDCOL = D, D + E
EPS = 1e-5
XSCALE = 2.0 ** 11
EXPO_MASK = 0x7F800000
EXPO_UNIT = 1 << 23
TOP = 14
RB = 3
U = 4
LOOPS = NT // U
WCOLS = KD * H


def build(nc, t):
    ctx = ExitStack()
    with ctx:
        def sb(name, shape, dt=F32):
            return ctx.enter_context(nc.sbuf_tensor(name, shape, dt))

        def sem(name):
            return ctx.enter_context(nc.semaphore(name))

        arena = sb("arena", [P, T * N])
        x_all = sb("x_all", [P, T, D])
        Y = sb("Y", [P, T, D])
        stage = sb("stage", [P, 2, WCOLS])
        b2r = sb("b2r", [P, E, D])
        gnnb = sb("gnnb", [P, D])
        W = sb("W", [P, KD, D])
        gw = sb("gw", [P, KD, E])
        gb = sb("gb", [P, E])
        b1 = sb("b1", [P, E, HT])
        xn = sb("xn", [P, 2, D])
        xnT = sb("xnT", [P, 2, D])
        x1 = sb("x1", [P, 2, D])
        row = sb("row", [P, RB, ROW])
        red = sb("red", [P, 2, P])
        scratch = sb("scratch", [P, WCOLS // 2])
        pad = sb("pad", [P, ROW])
        identf = sb("identf", [P, P])
        identh = sb("identh", [P, P], F16)
        onesf = sb("onesf", [P, P])
        onesb = sb("onesb", [P, P], BF16)
        before = sb("before", [P, P], BF16)
        eps = sb("eps", [P, 1])
        zero = sb("zero", [P, 1])
        iota8 = sb("iota8", [P, E])
        eoff = sb("eoff", [P, E])
        tokid = sb("tokid", [P, T])
        iotat = sb("iotat", [P, NT])
        stats = sb("stats", [P, T, 6])
        mv = sb("mv", [P, T, 2])
        std = sb("std", [P, T])
        rstd = sb("rstd", [P, T])
        dmax = sb("dmax", [P, T])
        dsq = sb("dsq", [P, T])
        drec = sb("drec", [P, T])
        dinv = sb("dinv", [P, T])
        stats2 = sb("stats2", [P, 2, 6])
        mv2 = sb("mv2", [P, 2, 2])
        std2 = sb("std2", [P, 2, 1])
        rstd2 = sb("rstd2", [P, 2, 1])
        lg = sb("lg", [P, 2, E])
        top8 = sb("top8", [P, 2, E])
        idx8 = sb("idx8", [P, E], U32)
        idxf = sb("idxf", [P, 2])
        oh = sb("oh", [P, 2, TOPK, E])
        mask = sb("mask", [P, 2, E], BF16)
        cum = sb("cum", [P, T + 1, E], BF16)
        negm = sb("negm", [P, 2, 1])
        ex = sb("ex", [P, 2, E])
        sumex = sb("sumex", [P, 2, 1])
        rsum = sb("rsum", [P, 2, 1])
        base = sb("base", [P, E])
        tmp8 = sb("tmp8", [P, TOPK, E])
        slotf = sb("slotf", [P, TOPK])
        slot = sb("slot", [P, RB, TOPK], U32)
        ss = sb("ss", [P, E, 3])
        nsum = sb("nsum", [P, 3])
        ntmp = sb("ntmp", [P, 1])
        nroot = sb("nroot", [P, 3])
        nclip = sb("nclip", [P, 3])
        pw = sb("pw", [P, 3], I32)
        sc = sb("sc", [P, E, 3], I32)
        inv1 = sb("inv1", [P, E])
        inv2 = sb("inv2", [P, E])
        tl = sb("tl", [P, 6, E])
        tli = sb("tli", [P, 2, E], I32)
        etab = sb("etab", [1, NT], I32)
        rtab = sb("rtab", [1, NT], I32)
        ptab = sb("ptab", [1, E], I32)
        idu = sb("idu", [P, U, 1], U32)
        gs = sb("gs", [P, 2, 1])
        PS = ctx.enter_context(nc.psum_tensor("PS", [P, 8, 512], F32))

        arena_h = arena[:, :].bitcast(F16)
        wv = arena_h.rearrange("p (e q n) -> p e q n", e=E, q=4)
        junk = scratch[:, :].bitcast(BF16)
        cmp = scratch[0:1, 0:2 * E * NT].rearrange("p (q e t) -> p q e t", q=2, e=E)
        xflat = x_all[:, :, :].rearrange("p t d -> p (t d)")
        yflat = Y[:, :, :].rearrange("p t d -> p (t d)")
        g = xflat[:, 0:2 * H].rearrange("p (b n) -> p b n", b=2)
        hs = xflat[:, 2 * H:4 * H].bitcast(F16).rearrange("p (b q n) -> p b q n", b=2, q=2)
        xrow = yflat[:, 0:U * ROW].rearrange("p (b n) -> p b n", b=U)
        y0 = U * ROW
        xT = yflat[:, y0:y0 + 2 * D].bitcast(F16).rearrange("p (b n) -> p b n", b=2)
        yout = yflat[:, y0 + 2 * D:y0 + 4 * D].rearrange("p (b n) -> p b n", b=2)

        yb = yflat[:, y0 + 4 * D:y0 + 6 * D].rearrange("p (b n) -> p b n", b=2)
        lin = W[:, 0, :]
        tt = lin[0:1, 0:6 * NT].rearrange("p (q t) -> p q t", q=6)

        xs = nc.dram_tensor("xs", (EMPTY + P, ROW), F32).ap()
        out = t["out"]

        x_in, small_in = sem("x_in"), sem("small_in")
        adj_in = [sem(f"adj_in{i}") for i in range(T)]
        w_in = [sem("w1_in"), sem("w2_in")]
        const_chain, consts = sem("const_chain"), sem("consts")
        dve_chain = sem("dve_chain")
        var_ready, std_ready = sem("var_ready"), sem("std_ready")
        xn_ready, xnT_psum, xnT_ready = sem("xn_ready"), sem("xnT_psum"), sem("xnT_ready")
        Y_psum, Y_ready, Y_scaled = sem("Y_psum"), sem("Y_ready"), sem("Y_scaled")
        red_ready, rowsum_ready = sem("red_ready"), sem("rowsum_ready")
        deg_ready, deg_root = sem("deg_ready"), sem("deg_root")
        agg_ready, lin_done, x1_ready, x1_stored = (
            sem("agg_ready"), sem("lin_done"), sem("x1_ready"), [sem("x1_stored0"), sem("x1_stored1")])
        var2_ready, std2_ready = sem("var2_ready"), sem("std2_ready")
        logits_psum, logits_read = sem("logits_psum"), sem("logits_read")
        cum_ready, rank_psum, rank_read = sem("cum_ready"), sem("rank_psum"), sem("rank_read")
        negm_ready, exp_ready = sem("negm_ready"), sem("exp_ready")
        slot_ready, scattered = sem("slot_ready"), sem("scattered")
        squares, norm_psum, norm_sum, norm_root = (
            sem("squares"), sem("norm_psum"), sem("norm_sum"), sem("norm_root"))
        scale_ready, hi_ready, lo_ready = sem("scale_ready"), sem("hi_ready"), sem("lo_ready")
        count_psum, tables, pads_in = sem("count_psum"), sem("tables"), sem("pads_in")
        xrow_in = [sem(f"xrow_in{j}") for j in range(U)]
        xT_psum, xT_ready = sem("xT_psum"), sem("xT_ready")
        h_psum, g_ready, h_hi, h_split = sem("h_psum"), sem("g_ready"), sem("h_hi"), sem("h_split")
        y_psum, yb_ready, gs_ready, y_ready = (
            sem("y_psum"), sem("yb_ready"), sem("gs_ready"), sem("y_ready"))
        added = sem("added")
        pool_step = sem("pool_step")
        act_step, dve_step = sem("act_step"), sem("dve_step")

        block = ctx.enter_context(nc.Block())

        def tiles(body):
            def run(eng):
                for j in range(U):
                    body(0, j)
                with eng.Fori(1, LOOPS) as u:
                    for j in range(U):
                        body(u, j)
                for j in range(NT - U * LOOPS):
                    body(LOOPS, j)
            return run

        def later(u, j, n):
            u, j = u + (j + n) // U, (j + n) % U
            if isinstance(u, int) and U * u + j >= NT:
                return None
            return u, j

        @block.sync
        def _(sp):
            sp.dma_start(x_all[:, :, :], t["x"]).then_inc(x_in, 16)
            for i in range(T):
                sp.dma_start(arena[:, i * N:(i + 1) * N], t["adjT"][i]).then_inc(adj_in[i], 16)
            sp.wait_ge(consts, 1)
            sp.dma_start(xs[EMPTY:EMPTY + P, :], pad[:, :]).then_inc(pads_in, 16)
            sp.dma_start(out[N:N + P, :], pad[:, 0:D]).then_inc(pads_in, 16)

            def load_expert(e):
                if e:
                    sp.wait_ge(lo_ready, 2 * e)
                sp.dma_start(stage[:, 0, :], t["w1"][e]).then_inc(w_in[0], 16)
                sp.dma_start(stage[:, 1, :], t["w2"][e]).then_inc(w_in[1], 16)

            load_expert(0)
            for i in range(T):
                sp.wait_ge(x1_ready, i + 1)
                sp.dma_start(out[i * P:(i + 1) * P, :], x1[:, i % 2, :])\
                  .then_inc(x1_stored[i % 2], 16)
                if i % 2 and i // 2 + 1 < E:
                    load_expert(i // 2 + 1)
            sp.wait_ge(tables, 1)
            for e in range(E):
                r = sp.value_load(ptab[0:1, e:e + 1], min_val=0, max_val=EMPTY - P)
                sp.dma_start(xs[bass.ds(r, P), :], pad[:, :]).then_inc(pads_in, 16)
            sp.wait_ge(pads_in, 16 * (E + 2))
            sp.wait_ge(scattered, 16 * TOPK * T)
            sp.wait_ge(agg_ready, T)

            def load_rows(u, j):
                if not (isinstance(u, int) and u == 0):
                    sp.wait_ge(added, (u - 1) * U * 16 + (j + 1) * 16)
                r = sp.value_load(rtab[0:1, bass.ds(u * U + j, 1)], min_val=0, max_val=EMPTY)
                sp.dma_start(xrow[:, j, :], xs[bass.ds(r, P), :]).then_inc(xrow_in[j], 16)

            tiles(load_rows)(sp)

        @block.gpsimd
        def _(pool):
            n = [0]

            def link(ins):
                n[0] += 1
                ins.then_inc(const_chain, 1)
                pool.wait_ge(const_chain, n[0])

            pool.memset(identf[:, :], 0.0)
            pool.memset(identh[:, :], 0.0)
            pool.memset(onesf[:, :], 1.0)
            pool.memset(onesb[:, :], 1.0)
            pool.memset(before[:, :], 0.0)
            pool.memset(eps[:, :], EPS)
            pool.memset(zero[:, :], 0.0)
            pool.memset(cum[:, 0, :], 0.0)
            link(pool.memset(pad[:, :], 0.0))
            for m in (identf, identh):
                pool.affine_select(out=m[:, :], in_=m[:, :], compare_op=ALU.not_equal, fill=1.0,
                                   base=0, pattern=[[-1, P]], channel_multiplier=1)
            pool.affine_select(out=before[:, :], in_=before[:, :], compare_op=ALU.is_ge, fill=1.0,
                               base=0, pattern=[[-1, P]], channel_multiplier=1)

            def iota(o, pattern, b, m):
                return pool.iota(o, pattern=pattern, base=b, channel_multiplier=m,
                                 allow_small_or_imprecise_dtypes=True)

            iota(iota8[:, :], [[1, E]], 0, 0)
            iota(eoff[:, :], [[REGION, E]], 0, 0)
            iota(tokid[:, :], [[P, T]], 0, 1)
            iota(iotat[:, :], [[1, NT]], 0, 0)
            iota(pad[:, IDCOL:IDCOL + 1], [[0, 1]], N, 1).then_inc(consts, 1)

            for i in range(T):
                pool.wait_ge(slot_ready, i + 1)
                for k in range(TOPK):
                    pool.indirect_dma_start(
                        xs[:, :], bass.IndirectOffsetOnAxis(ap=slot[:, i % RB, k:k + 1], axis=0),
                        row[:, i % RB, :], None).then_inc(scattered, 16)

            for b in range(2):
                pool.wait_ge(x1_stored[b], 16 * T // 2)
            pool.wait_ge(pads_in, 16 * (E + 2))

            def add_rows(u, j):
                first = isinstance(u, int) and u == 0 and j == 0
                if not first:
                    pool.wait_ge(added, (u * U + j) * 16)
                    pool.sem_inc(pool_step, 1)
                pool.wait_ge(y_ready, u * U + j + 1)
                pool.sem_inc(pool_step, 1)
                pool.indirect_dma_start(
                    out[:, :], bass.IndirectOffsetOnAxis(ap=idu[:, j, :], axis=0),
                    yout[:, j % 2, :], None, compute_op=ALU.add).then_inc(added, 16)

            tiles(add_rows)(pool)
            pool.wait_ge(added, 16 * NT)

        @block.scalar
        def _(act):
            for dst, src in ((W, "W"), (gw, "gate_w"), (b1, "b1"), (b2r, "b2")):
                act.dma_start(dst[:, :, :], t[src]).then_inc(small_in, 16)
            for dst, src in ((gb, "gate_b"), (gnnb, "gnn_b")):
                act.dma_start(dst[:, :], t[src]).then_inc(small_in, 16)

            act.wait_ge(var_ready, 1)
            act.wait_ge(consts, 1)
            act.activation(std[:, :], mv[:, :, 1], ACT.Sqrt, bias=eps[:, :]).then_inc(std_ready, 1)

            def copy_xnT(n):
                act.wait_ge(xnT_psum, n + 1)
                if n >= 2:
                    if n - 2 < T:
                        act.wait_ge(Y_psum, n - 1)
                    else:
                        act.wait_ge(logits_psum, n - T - 1)
                act.activation(xnT[:, n % 2, :], PS[:, 2 + n % 2, 0:D], ACT.Copy)\
                   .then_inc(xnT_ready, 1)

            def copy_Y(i):
                act.wait_ge(Y_psum, i + 1)
                act.activation(Y[:, i, :], PS[:, i % 2, 0:D], ACT.Copy).then_inc(Y_ready, 1)

            def deg(q):
                act.wait_ge(deg_ready, q + 1)
                act.activation(dsq[:, 4 * q:4 * q + 4], dmax[:, 4 * q:4 * q + 4], ACT.Sqrt)\
                   .then_inc(deg_root, 1)

            for i in range(T + 1):
                if i < T:
                    copy_xnT(i)
                if i:
                    copy_Y(i - 1)
                if i and i % 4 == 0:
                    deg(i // 4 - 1)

            def square_sums(e):
                if e == 0:
                    act.wait_ge(small_in, 16 * 6)
                for q in range(2):
                    act.wait_ge(w_in[q], 16 * (e + 1))
                    if e or q:
                        act.wait_ge(squares, 3 * e + q)
                    act.activation(junk, stage[:, q, :], ACT.Square,
                                   accum_out=ss[:, e, q:q + 1]).then_inc(squares, 1)
                act.wait_ge(squares, 3 * e + 2)
                act.activation(junk[:, 0:HT], b1[:, e, :], ACT.Square,
                               accum_out=ss[:, e, 2:3]).then_inc(squares, 1)

            def norm_roots(e):
                act.wait_ge(norm_sum, e + 1)
                act.activation(nroot[:, :], nsum[:, :], ACT.Sqrt).then_inc(norm_root, 1)

            def hi_parts(e):
                act.wait_ge(scale_ready, e + 1)
                act.wait_ge(agg_ready, 2 * e + 2)
                for q in range(2):
                    act.activation(wv[:, e, 2 * q, :], stage[:, q, :], ACT.Copy,
                                   scale=sc[:, e, q:q + 1].bitcast(F32)).then_inc(hi_ready, 1)

            for i in range(T + 2):
                if i < T:
                    act.wait_ge(var2_ready, i + 1)
                    act.activation(std2[:, i % 2, :], mv2[:, i % 2, 1:2], ACT.Sqrt,
                                   bias=eps[:, :]).then_inc(std2_ready, 1)
                if 1 <= i <= T:
                    copy_xnT(T + i - 1)
                if i % 2 == 0 and i // 2 < E:
                    square_sums(i // 2)
                    norm_roots(i // 2)
                if 1 <= i <= T:
                    act.wait_ge(negm_ready, i)
                    act.activation(ex[:, (i - 1) % 2, :], lg[:, (i - 1) % 2, :], ACT.Exp,
                                   bias=negm[:, (i - 1) % 2, :],
                                   accum_out=sumex[:, (i - 1) % 2, :]).then_inc(exp_ready, 1)
                if i % 2 and i // 2 < E:
                    hi_parts(i // 2)

            def copy_xT(u, j):
                act.wait_ge(xT_psum, u * U + j + 1)
                act.sem_inc(act_step, 1)
                if not (isinstance(u, int) and u * U + j < 2):
                    act.wait_ge(h_psum, 2 * (u * U + j) - 2)
                    act.sem_inc(act_step, 1)
                act.activation(xT[:, j % 2, :], PS[:, 6 + j % 2, 0:D].bitcast(F16), ACT.Copy)\
                   .then_inc(xT_ready, 1)

            def gelus(u, j):
                e = act.value_load(etab[0:1, bass.ds(u * U + j, 1)], min_val=0, max_val=E - 1)
                for q in range(2):
                    act.wait_ge(h_psum, 2 * (u * U + j) + q + 1)
                    act.sem_inc(act_step, 1)
                    if q == 0 and not (isinstance(u, int) and u * U + j < 2):
                        act.wait_ge(h_split, 2 * (u * U + j) - 2)
                        act.sem_inc(act_step, 1)
                    for h in range(q * HT // 2, (q + 1) * HT // 2):
                        last = act.activation(
                            g[:, j % 2, h * P:(h + 1) * P],
                            PS[:, 2 * (j % 2) + q, (h % (HT // 2)) * P:(h % (HT // 2) + 1) * P],
                            ACT.Gelu,
                            bias=b1[:, bass.ds(e, 1), h:h + 1].rearrange("p a b -> p (a b)"),
                            scale=inv1[:, bass.ds(e, 1)])
                    last.then_inc(g_ready, 1)

            act.wait_ge(tables, 1)
            copy_xT(0, 0)
            copy_xT(0, 1)
            gelus(0, 0)

            def body(u, j):
                if nxt := later(u, j, 1):
                    gelus(*nxt)
                if nxt := later(u, j, 2):
                    copy_xT(*nxt)

            tiles(body)(act)

        @block.vector
        def _(dve):
            n = [0]

            def link(ins):
                n[0] += 1
                ins.then_inc(dve_chain, 1)
                dve.wait_ge(dve_chain, n[0])

            dve.wait_ge(x_in, 16)
            for i in range(T):
                last = dve.bn_stats(stats[:, i, :], x_all[:, i, :])
            link(last)
            for i in range(T):
                last = dve.bn_aggr(mv[:, i, :], stats[:, i, :])
            last.then_inc(var_ready, 1)
            dve.wait_ge(std_ready, 1)
            link(dve.reciprocal(rstd[:, :], std[:, :]))

            def degrees(q):
                c = slice(4 * q, 4 * q + 4)
                dve.wait_ge(rowsum_ready, 4 * q + 4)
                dve.tensor_scalar(dmax[:, c], PS[:, 6, c], 2.0 ** -116, None, ALU.max)\
                   .then_inc(deg_ready, 1)
                dve.wait_ge(deg_root, q + 1)
                link(dve.reciprocal(drec[:, c], dsq[:, c]))
                link(dve.scalar_tensor_tensor(dinv[:, c], PS[:, 6, c], 0.0, drec[:, c],
                                              ALU.is_gt, ALU.mult))
                dve.wait_ge(Y_ready, 4 * q + 4)
                for k in range(4 * q, 4 * q + 4):
                    dve.tensor_scalar(Y[:, k, :], Y[:, k, :], dinv[:, k:k + 1], None,
                                      ALU.mult).then_inc(Y_scaled, 1)

            for i in range(T + 1):
                if i < T:
                    if i >= 2:
                        dve.wait_ge(xnT_psum, i - 1)
                    dve.tensor_scalar(xn[:, i % 2, :], x_all[:, i, :], mv[:, i, 0:1],
                                      rstd[:, i:i + 1], ALU.subtract, ALU.mult)\
                       .then_inc(xn_ready, 1)
                    dve.wait_ge(adj_in[i], 16)
                    if i >= 2:
                        dve.wait_ge(rowsum_ready, i - 1)
                    dve.tensor_reduce(
                        red[:, i % 2, :],
                        arena[:, i * N:(i + 1) * N].rearrange("p (k c) -> p c k", k=T),
                        AX.X, ALU.add).then_inc(red_ready, 1)
                if i and i % 4 == 0:
                    degrees(i // 4 - 1)

            dve.wait_ge(small_in, 16 * 6)

            def new_x(i):
                b = i % 2
                dve.wait_ge(agg_ready, i + 1)
                dve.scalar_tensor_tensor(lin[:, :], PS[:, b, 0:D], dinv[:, i:i + 1], gnnb[:, :],
                                         ALU.mult, ALU.add).then_inc(lin_done, 1)
                dve.wait_ge(lin_done, i + 1)
                if i >= 2:
                    dve.wait_ge(x1_stored[b], 16 * (i // 2))
                dve.scalar_tensor_tensor(x1[:, b, :], lin[:, :], 0.0, x_all[:, i, :],
                                         ALU.max, ALU.add).then_inc(x1_ready, 1)
                dve.wait_ge(x1_ready, i + 1)
                link(dve.bn_stats(stats2[:, b, :], x1[:, b, :]))
                dve.bn_aggr(mv2[:, b, :], stats2[:, b, :]).then_inc(var2_ready, 1)

            def normalise(i):
                b = i % 2
                dve.wait_ge(std2_ready, i + 1)
                link(dve.reciprocal(rstd2[:, b, :], std2[:, b, :]))
                dve.wait_ge(xnT_psum, T + i - 1)
                dve.tensor_scalar(xn[:, b, :], x1[:, b, :], mv2[:, b, 0:1], rstd2[:, b, :],
                                  ALU.subtract, ALU.mult).then_inc(xn_ready, 1)
                dve.wait_ge(xn_ready, T + i + 1)
                if i >= RB:
                    dve.wait_ge(scattered, 16 * TOPK * (i - RB + 1))
                words = row[:, i % RB, 0:D].bitcast(F16)
                link(dve.tensor_scalar(words[:, 0:D], xn[:, b, :], XSCALE, None, ALU.mult))
                dve.scalar_tensor_tensor(words[:, D:2 * D], xn[:, b, :], XSCALE, words[:, 0:D],
                                         ALU.mult, ALU.subtract)
                dve.tensor_copy(row[:, i % RB, IDCOL:IDCOL + 1], tokid[:, i:i + 1])

            def choose(i):
                b = i % 2
                dve.wait_ge(logits_psum, i + 1)
                dve.tensor_tensor(lg[:, b, :], PS[:, 4, 0:E], gb[:, :], ALU.add)\
                   .then_inc(logits_read, 1)
                dve.wait_ge(logits_read, i + 1)
                link(dve.max(top8[:, b, :], lg[:, b, :]))
                dve.tensor_scalar(negm[:, b, :], top8[:, b, 0:1], -1.0, None, ALU.mult)\
                   .then_inc(negm_ready, 1)
                link(dve.max_index(idx8[:, :], top8[:, b, :], lg[:, b, :]))
                link(dve.tensor_copy(idxf[:, :], idx8[:, 0:TOPK]))
                for k in range(TOPK):
                    last = dve.tensor_scalar(oh[:, b, k, :], iota8[:, :], idxf[:, k:k + 1], None,
                                             ALU.is_equal)
                link(last)
                link(dve.tensor_tensor(mask[:, b, :], oh[:, b, 0, :], oh[:, b, 1, :], ALU.add))
                dve.tensor_tensor(cum[:, i + 1, :], cum[:, i, :], mask[:, b, :], ALU.add)\
                   .then_inc(cum_ready, 1)

            def gates(i):
                b = i % 2
                dve.wait_ge(exp_ready, i + 1)
                link(dve.reciprocal(rsum[:, b, :], sumex[:, b, :]))
                link(dve.scalar_tensor_tensor(row[:, i % RB, GATE0:GATE0 + E], ex[:, b, :],
                                              rsum[:, b, :], mask[:, b, :], ALU.mult, ALU.mult))

            def slots(i):
                b = i % 2
                dve.wait_ge(rank_psum, i + 1)
                dve.tensor_tensor(base[:, :], PS[:, 5, 0:E], eoff[:, :], ALU.add)\
                   .then_inc(rank_read, 1)
                dve.wait_ge(rank_read, i + 1)
                for k in range(TOPK):
                    last = dve.tensor_tensor_reduce(tmp8[:, k, :], oh[:, b, k, :], base[:, :],
                                                    1.0, 0.0, ALU.mult, ALU.add, slotf[:, k:k + 1])
                link(last)
                if i >= RB:
                    dve.wait_ge(scattered, 16 * TOPK * (i - RB + 1))
                dve.tensor_copy(slot[:, i % RB, :], slotf[:, :]).then_inc(slot_ready, 1)

            def scales(e):
                dve.wait_ge(norm_psum, e + 1)
                link(dve.tensor_scalar(ntmp[:, :], PS[:, 7, 2:3], 2.0, None, ALU.mult))
                dve.tensor_copy(nsum[:, 0:2], PS[:, 7, 0:2])
                dve.scalar_tensor_tensor(nsum[:, 2:3], PS[:, 7, 0:1], 2.0 * D, ntmp[:, :],
                                         ALU.mult, ALU.add).then_inc(norm_sum, 1)
                dve.wait_ge(norm_root, e + 1)
                link(dve.tensor_scalar(nclip[:, :], nroot[:, :], 2.0 ** -60, None, ALU.max))
                link(dve.tensor_scalar(pw[:, :], nclip[:, :].bitcast(I32), EXPO_MASK, None,
                                       ALU.bitwise_and))
                pf = pw[:, :].bitcast(F32)
                dve.tensor_scalar(inv1[:, e:e + 1], pf[:, 0:1], 2.0 ** -TOP / XSCALE, None,
                                  ALU.mult)
                dve.scalar_tensor_tensor(inv2[:, e:e + 1], pf[:, 1:2], 2.0 ** (-2 * TOP),
                                         pf[:, 2:3], ALU.mult, ALU.mult)
                dve.tensor_scalar(sc[:, e, :], pw[:, :], -1.0, float((254 + TOP) * EXPO_UNIT),
                                  ALU.mult, ALU.add).then_inc(scale_ready, 1)

            def lo_parts(e):
                for q in range(2):
                    dve.wait_ge(hi_ready, 2 * e + q + 1)
                    dve.scalar_tensor_tensor(wv[:, e, 2 * q + 1, :], stage[:, q, :],
                                             sc[:, e, q:q + 1].bitcast(F32), wv[:, e, 2 * q, :],
                                             ALU.mult, ALU.subtract).then_inc(lo_ready, 1)

            for i in range(T + 2):
                if i < T:
                    new_x(i)
                if 1 <= i <= T:
                    choose(i - 1)
                if i < T:
                    normalise(i)
                if i >= 2:
                    slots(i - 2)
                if i % 2 == 0 and i // 2 < E:
                    scales(i // 2)
                if 1 <= i <= T:
                    gates(i - 1)
                if i % 2 and i // 2 < E:
                    lo_parts(i // 2)

            dve.wait_ge(count_psum, 1)
            cnt = PS[:, 7, 8:8 + E]
            dve.tensor_scalar(tli[:, 0, :], cnt, float(P - 1), None, ALU.add)
            link(dve.tensor_tensor(ptab[0:1, :], PS[0:1, 7, 8:8 + E], eoff[0:1, :], ALU.add))
            link(dve.tensor_scalar(tli[:, 1, :], tli[:, 0, :], P.bit_length() - 1, None,
                                   ALU.logical_shift_right))
            link(dve.tensor_copy(tl[:, 0, :], tli[:, 1, :]))
            link(dve.tensor_tensor_scan(tl[:, 1, :], onesf[:, 0:E], tl[:, 0, :], 0.0,
                                        ALU.mult, ALU.add))
            for e in range(E):
                dve.tensor_scalar(cmp[:, 0, e, :], iotat[0:1, :], tl[0:1, 1, e:e + 1], None,
                                  ALU.is_ge)
                last = dve.tensor_scalar(cmp[:, 1, e, :], iotat[0:1, :], tl[0:1, 1, e:e + 1],
                                         tl[0:1, 0, e:e + 1], ALU.is_ge, ALU.mult)
            link(last)
            for q in range(2):
                last = dve.tensor_reduce(tt[:, q, :], cmp[:, q, :, :].rearrange("p e t -> p t e"),
                                         AX.X, ALU.add)
            link(last)
            link(dve.tensor_tensor(tt[:, 2, :], iotat[0:1, :], tt[:, 1, :], ALU.subtract))
            link(dve.tensor_scalar(tt[:, 3, :], tt[:, 2, :], float(P), None, ALU.mult))
            link(dve.scalar_tensor_tensor(tt[:, 4, :], tt[:, 0, :], float(REGION), tt[:, 3, :],
                                          ALU.mult, ALU.add))
            dve.tensor_scalar(etab[:, :], tt[:, 0, :], float(E - 1), None, ALU.min)
            dve.tensor_scalar(rtab[:, :], tt[:, 4, :], float(EMPTY), None, ALU.min)\
               .then_inc(tables, 1)

            dve.wait_ge(tables, 1)
            def split(u, j):
                e = dve.value_load(etab[0:1, bass.ds(u * U + j, 1)], min_val=0, max_val=E - 1)
                s = sc[:, :, :].bitcast(F32)[:, bass.ds(e, 1), 2:3].rearrange("p a b -> p (a b)")
                half = H // 2
                for q in range(2):
                    cols = slice(q * half, (q + 1) * half)
                    dve.wait_ge(g_ready, 2 * (u * U + j) + q + 1)
                    dve.sem_inc(dve_step, 1)
                    if q == 0 and not (isinstance(u, int) and u * U + j < 2):
                        dve.wait_ge(y_psum, u * U + j - 1)
                        dve.sem_inc(dve_step, 1)
                    dve.tensor_scalar(hs[:, j % 2, 0, cols], g[:, j % 2, cols], s, None,
                                      ALU.mult).then_inc(h_hi, 1)
                    dve.wait_ge(h_hi, 2 * (u * U + j) + q + 1)
                    dve.sem_inc(dve_step, 1)
                    dve.scalar_tensor_tensor(hs[:, j % 2, 1, cols], g[:, j % 2, cols], s,
                                             hs[:, j % 2, 0, cols], ALU.mult, ALU.subtract)\
                       .then_inc(h_split, 1)

            def result(u, j):
                tau = u * U + j
                e = dve.value_load(etab[0:1, bass.ds(tau, 1)], min_val=0, max_val=E - 1)
                gate = xrow[:, j, GATE0:GATE0 + E][:, bass.ds(e, 1)]
                dve.wait_ge(xrow_in[j], (u + 1) * 16)
                dve.sem_inc(dve_step, 1)
                if not (isinstance(u, int) and tau < 2):
                    dve.wait_ge(added, (tau - 1) * 16)
                    dve.sem_inc(dve_step, 1)
                dve.tensor_copy(idu[:, j, :], xrow[:, j, IDCOL:IDCOL + 1])
                dve.tensor_tensor(gs[:, j % 2, :], gate, inv2[:, bass.ds(e, 1)], ALU.mult)\
                   .then_inc(gs_ready, 1)
                dve.tensor_scalar(yb[:, j % 2, :],
                                  b2r[:, bass.ds(e, 1), :].rearrange("p a b -> p (a b)"),
                                  gate, None, ALU.mult).then_inc(yb_ready, 1)
                dve.wait_ge(gs_ready, tau + 1)
                dve.sem_inc(dve_step, 1)
                dve.wait_ge(yb_ready, tau + 1)
                dve.sem_inc(dve_step, 1)
                dve.wait_ge(y_psum, tau + 1)
                dve.sem_inc(dve_step, 1)
                dve.scalar_tensor_tensor(yout[:, j % 2, :], PS[:, 4 + j % 2, 0:D], gs[:, j % 2, :],
                                         yb[:, j % 2, :], ALU.mult, ALU.add).then_inc(y_ready, 1)

            split(0, 0)

            def body(u, j):
                if nxt := later(u, j, 1):
                    split(*nxt)
                result(u, j)

            tiles(body)(dve)

        @block.tensor
        def _(pe):
            def transposes(n):
                pe.wait_ge(xn_ready, n + 1)
                if n >= 2:
                    pe.wait_ge(xnT_ready, n - 1)
                for k in range(KD):
                    last = pe.transpose(PS[:, 2 + n % 2, k * P:(k + 1) * P],
                                        xn[:, n % 2, k * P:(k + 1) * P], identf[:, :])
                last.then_inc(xnT_psum, 1)

            def product_W(i):
                pe.wait_ge(xnT_ready, i + 1)
                if i >= 2:
                    pe.wait_ge(Y_ready, i - 1)
                for k in range(KD):
                    last = pe.matmul(PS[:, i % 2, 0:D], xnT[:, i % 2, k * P:(k + 1) * P],
                                     W[:, k, :], start=(k == 0), stop=(k == KD - 1))
                last.then_inc(Y_psum, 1)

            def rowsum(i):
                pe.wait_ge(red_ready, i + 1)
                pe.matmul(PS[:, 6, i:i + 1], red[:, i % 2, :], onesf[:, 0:1], start=True,
                          stop=True).then_inc(rowsum_ready, 1)

            pe.wait_ge(consts, 1)
            pe.wait_ge(small_in, 16 * 6)
            for i in range(T + 1):
                if i < T:
                    transposes(i)
                if i:
                    product_W(i - 1)
                    rowsum(i - 1)

            def adj_product(i, ks):
                if ks[0] == 0:
                    if i >= 2:
                        pe.wait_ge(lin_done, i - 1)
                    if i == 0:
                        pe.wait_ge(Y_ready, T)
                for k in ks:
                    if i == 0:
                        pe.wait_ge(Y_scaled, k + 1)
                    c = i * N + k * P
                    last = pe.matmul(PS[:, i % 2, 0:D], arena[:, c:c + P], Y[:, k, :],
                                     start=(k == 0), stop=(k == T - 1))
                if ks[-1] == T - 1:
                    last.then_inc(agg_ready, 1)

            def logits(i):
                pe.wait_ge(xnT_ready, T + i + 1)
                if i:
                    pe.wait_ge(logits_read, i)
                for k in range(KD):
                    last = pe.matmul(PS[:, 4, 0:E], xnT[:, i % 2, k * P:(k + 1) * P], gw[:, k, :],
                                     start=(k == 0), stop=(k == KD - 1))
                last.then_inc(logits_psum, 1)

            def ranks(i):
                pe.wait_ge(cum_ready, i + 1)
                if i:
                    pe.wait_ge(rank_read, i)
                pe.matmul(PS[:, 5, 0:E], before[:, :], mask[:, i % 2, :], start=True, stop=False)
                pe.matmul(PS[:, 5, 0:E], onesb[:, :], cum[:, i, :], start=False, stop=True)\
                  .then_inc(rank_psum, 1)

            def norms(e):
                pe.wait_ge(squares, 3 * e + 3)
                if e:
                    pe.wait_ge(norm_sum, e)
                pe.matmul(PS[:, 7, 0:3], onesf[:, :], ss[:, e, :], start=True, stop=True)\
                  .then_inc(norm_psum, 1)

            for i in range(T + 2):
                if i < T:
                    adj_product(i, range(T // 2))
                if 1 <= i <= T:
                    transposes(T + i - 1)
                if i >= 2:
                    ranks(i - 2)
                if i < T:
                    adj_product(i, range(T // 2, T))
                if i % 2 == 0 and i // 2 < E:
                    norms(i // 2)
                if 1 <= i <= T:
                    logits(i - 1)
            pe.matmul(PS[:, 7, 8:8 + E], onesb[:, :], cum[:, T, :], start=True, stop=True)\
              .then_inc(count_psum, 1)

            pe.wait_ge(rank_read, T)
            pe.wait_ge(lo_ready, 2 * E)

            def expert(u, j):
                return pe.value_load(etab[0:1, bass.ds(u * U + j, 1)], min_val=0, max_val=E - 1)

            def weights(e, q, c, n):
                return wv[:, bass.ds(e, 1), q, c:c + n].rearrange("p a b -> p (a b)")

            def turn_rows(u, j):
                pe.wait_ge(xrow_in[j], (u + 1) * 16)
                if not (isinstance(u, int) and u * U + j < 2):
                    pe.wait_ge(xT_ready, u * U + j - 1)
                words = xrow[:, j, 0:D].bitcast(F16)
                for k in range(2 * KD):
                    last = pe.transpose(PS[:, 6 + j % 2, 0:D].bitcast(F16)[:, k * P:(k + 1) * P],
                                        words[:, k * P:(k + 1) * P], identh[:, :])
                last.then_inc(xT_psum, 1)

            def up(u, j):
                e = expert(u, j)
                pe.wait_ge(xT_ready, u * U + j + 1)
                if not (isinstance(u, int) and u * U + j < 2):
                    pe.wait_ge(g_ready, 2 * (u * U + j) - 2)
                for h in range(HT):
                    o = PS[:, 2 * (j % 2) + h // 4, (h % 4) * P:(h % 4 + 1) * P]
                    for k in range(KD):
                        c = k * H + h * P
                        x_hi = xT[:, j % 2, k * P:(k + 1) * P]
                        x_lo = xT[:, j % 2, (KD + k) * P:(KD + k + 1) * P]
                        pe.matmul(o, weights(e, 0, c, P), x_hi, start=(k == 0), stop=False)
                        pe.matmul(o, weights(e, 0, c, P), x_lo, start=False, stop=False)
                        last = pe.matmul(o, weights(e, 1, c, P), x_hi, start=False,
                                         stop=(k == KD - 1))
                    if h % 4 == 3:
                        last.then_inc(h_psum, 1)

            def down(u, j):
                e = expert(u, j)
                if not (isinstance(u, int) and u * U + j < 2):
                    pe.wait_ge(y_ready, u * U + j - 1)
                o = PS[:, 4 + j % 2, 0:D]
                for h in range(HT):
                    if h % 4 == 0:
                        pe.wait_ge(h_split, 2 * (u * U + j) + h // 4 + 1)
                    h_hi_, h_lo_ = (hs[:, j % 2, q, h * P:(h + 1) * P] for q in range(2))
                    pe.matmul(o, h_hi_, weights(e, 2, h * D, D), start=(h == 0), stop=False)
                    pe.matmul(o, h_hi_, weights(e, 3, h * D, D), start=False, stop=False)
                    last = pe.matmul(o, h_lo_, weights(e, 2, h * D, D), start=False,
                                     stop=(h == HT - 1))
                last.then_inc(y_psum, 1)

            pe.wait_ge(tables, 1)
            turn_rows(0, 0)
            turn_rows(0, 1)
            up(0, 0)

            def body(u, j):
                if nxt := later(u, j, 1):
                    up(*nxt)
                if nxt := later(u, j, 2):
                    turn_rows(*nxt)
                down(u, j)

            tiles(body)(pe)


def kernel(**inputs):
    import numpy as np
    import concourse.bacc as bacc
    from concourse.bass_utils import run_bass_kernel_spmd

    def rows(a, p=P):
        return np.broadcast_to(np.asarray(a).reshape(1, -1), (p, np.asarray(a).size))

    i = {k: np.asarray(v) for k, v in inputs.items()}
    arrays = {
        "x": i["x"].reshape(T, P, D).transpose(1, 0, 2),
        "adjT": i["adj"].reshape(T, P, T, P).transpose(0, 3, 2, 1).reshape(T, P, N),
        "W": i["L0_gnn_W"].reshape(KD, P, D).transpose(1, 0, 2),
        "gnn_b": rows(i["L0_gnn_b"]),
        "gate_w": i["L0_ffn_gate_w"].reshape(KD, P, E).transpose(1, 0, 2),
        "gate_b": rows(i["L0_ffn_gate_b"]),
        "w1": i["L0_ffn_w1"].reshape(E, KD, P, H).transpose(0, 2, 1, 3).reshape(E, P, WCOLS),
        "b1": i["L0_ffn_b1"].reshape(E, HT, P).transpose(2, 0, 1),
        "w2": i["L0_ffn_w2"].reshape(E, HT, P, D).transpose(0, 2, 1, 3).reshape(E, P, WCOLS),
        "b2": rows(i["L0_ffn_b2"]).reshape(P, E, D),
    }
    arrays = {f"{k}_in": np.ascontiguousarray(v) for k, v in arrays.items()}
    nc = bacc.Bacc("TRN2", target_bir_lowering=False, num_devices=1)
    t = {k[:-3]: nc.dram_tensor(k, v.shape, F32, kind="ExternalInput").ap()
         for k, v in arrays.items()}
    t["out"] = nc.dram_tensor("y_out", (N + P, D), F32, kind="ExternalOutput").ap()
    build(nc, t)
    r = run_bass_kernel_spmd(nc, [arrays], core_ids=[0])
    return r.results[0]["y_out"][:N]
```

```python
from contextlib import ExitStack

import concourse.bass as bass
from concourse import mybir

F32, F16, BF16 = mybir.dt.float32, mybir.dt.float16, mybir.dt.bfloat16
I32, U32 = mybir.dt.int32, mybir.dt.uint32
ACT, ALU, AX = mybir.ActivationFunctionType, mybir.AluOpType, mybir.AxisListType

P = 128
N, D, H, E, TOPK = 2048, 256, 1024, 8, 2
T = N // P
KD = D // P
HT = H // P
NT = TOPK * T + E - 1
REGION = N + P
EMPTY = E * REGION
ROW = D + E + 1
GATE0, IDCOL = D, D + E
EPS = 1e-5
XSCALE = 2.0 ** 11
EXPO_UNIT = 1 << 23
U = 4
EARLY = 4
ORDER = [0, 4, 1, 5, 2, 6, 3, 7, 8, 9, 10, 11, 12, 13, 14, 15]
BANKS = [0, 4, 0, 4, 1, 4, 1, 4, 0, 1, 4, 0, 1, 4, 0, 1]
HALF = [0, 0, 1, 0, 0, 0, 1, 0, 0, 0, 0, 0, 0, 0, 0, 0]
PREP = [0, 2, 1, 3, 4, 5, 6, 7]
RB = 3
LOOPS = NT // U
WCOLS = KD * H


def build(nc, t):
    ctx = ExitStack()
    with ctx:
        def sb(name, shape, dt=F32):
            return ctx.enter_context(nc.sbuf_tensor(name, shape, dt))

        def sem(name):
            return ctx.enter_context(nc.semaphore(name))

        arena = sb("arena", [P, T * N])
        x_all = sb("x_all", [P, T, D])
        Y = sb("Y", [P, T, D])
        stage = sb("stage", [P, 2, WCOLS])
        b2r = sb("b2r", [P, E, D])
        gnnb = sb("gnnb", [P, D])
        W = sb("W", [P, KD, D])
        gw = sb("gw", [P, KD, E])
        gb = sb("gb", [P, E])
        b1 = sb("b1", [P, E, HT])
        xn = sb("xn", [P, 2, D])
        xnT = sb("xnT", [P, 2, D])
        x1 = sb("x1", [P, 2, D])
        row = sb("row", [P, RB, ROW])
        red = sb("red", [P, 2, P])
        scratch = sb("scratch", [P, WCOLS // 2])
        pad = sb("pad", [P, ROW])
        identf = sb("identf", [P, P])
        identh = sb("identh", [P, P], F16)
        onesf = sb("onesf", [P, P])
        onesb = sb("onesb", [P, P], BF16)
        before = sb("before", [P, P], BF16)
        iota8 = sb("iota8", [P, E])
        eoff = sb("eoff", [P, E])
        tokid = sb("tokid", [P, T])
        iotat = sb("iotat", [P, NT])
        stats = sb("stats", [P, T, 6])
        mv = sb("mv", [P, T, 2])
        veps = sb("veps", [P, T])
        rstd = sb("rstd", [P, T])
        deg = sb("deg", [P, T])
        dmax = sb("dmax", [P, T])
        dpow = sb("dpow", [P, T])
        halves = sb("halves", [P, T])
        dinv = sb("dinv", [P, T])
        stats2 = sb("stats2", [P, 2, 6])
        mv2 = sb("mv2", [P, 2, 2])
        veps2 = sb("veps2", [P, 2, 1])
        rstd2 = sb("rstd2", [P, 2, 1])
        lg = sb("lg", [P, 2, E])
        top8 = sb("top8", [P, 2, E])
        idx8 = sb("idx8", [P, E], U32)
        idxf = sb("idxf", [P, 2])
        oh = sb("oh", [P, 2, TOPK, E])
        mask = sb("mask", [P, 2, E], BF16)
        cum = sb("cum", [P, T + 1, E], BF16)
        negm = sb("negm", [P, 2, 1])
        ex = sb("ex", [P, 2, E])
        sumex = sb("sumex", [P, 2, 1])
        rsum = sb("rsum", [P, 2, 1])
        base = sb("base", [P, E])
        tmp8 = sb("tmp8", [P, TOPK, E])
        slotf = sb("slotf", [P, TOPK])
        slot = sb("slot", [P, RB, TOPK], U32)
        ss = sb("ss", [P, E, 3])
        nsum = sb("nsum", [P, 3])
        ntmp = sb("ntmp", [P, 1])
        mexp = sb("mexp", [P, 3], I32)
        inv = sb("inv", [P, 3], I32)
        sc = sb("sc", [P, E, 3], I32)
        inv1 = sb("inv1", [P, E])
        inv2 = sb("inv2", [P, E])
        tl = sb("tl", [P, 6, E])
        tli = sb("tli", [P, 2, E], I32)
        etab = sb("etab", [1, NT], I32)
        rtab = sb("rtab", [1, NT], I32)
        ptab = sb("ptab", [1, E], I32)
        idu = sb("idu", [P, U, 1], U32)
        gs = sb("gs", [P, 2, 1])
        PS = ctx.enter_context(nc.psum_tensor("PS", [P, 8, 512], F32))

        halfwords = arena[:, :].bitcast(F16).rearrange("p (e w n) -> p e w n", e=E, w=2)
        w1v = halfwords[:, :, 0, :]
        w2v = halfwords[:, :, 1, :]

        def region(s):
            return PS[:, BANKS[s], HALF[s] * D:(HALF[s] + 1) * D]

        def turned(b):
            return PS[:, 2 + b, 0:D]

        def psum_Y(b):
            return PS[:, 4 + b, 0:D]

        def psum_sum(i):
            return PS[:, 6 + i % 2, 0:1]

        psum_norm, psum_rank = PS[:, 5, 0:3], PS[:, 7, 0:E]
        psum_logits, psum_count = PS[:, 6, 0:E], PS[:, 6, E:2 * E]

        def psum_h(h):
            return PS[:, h // 2, (h % 2) * P:(h % 2 + 1) * P]

        junk = scratch[:, :].bitcast(BF16)
        cmp = scratch[0:1, 0:2 * E * NT].rearrange("p (q e t) -> p q e t", q=2, e=E)
        xflat = x_all[:, :, :].rearrange("p t d -> p (t d)")
        yflat = Y[:, :, :].rearrange("p t d -> p (t d)")
        g = xflat[:, 0:2 * H].rearrange("p (b n) -> p b n", b=2)
        hs = xflat[:, 2 * H:4 * H].bitcast(F16).rearrange("p (b q n) -> p b q n", b=2, q=2)
        xrow = yflat[:, 0:U * ROW].rearrange("p (b n) -> p b n", b=U)
        y0 = U * ROW
        xT = yflat[:, y0:y0 + 2 * D].bitcast(F16).rearrange("p (b n) -> p b n", b=2)
        yout = yflat[:, y0 + 2 * D:y0 + 4 * D].rearrange("p (b n) -> p b n", b=2)

        yb = yflat[:, y0 + 4 * D:y0 + 6 * D].rearrange("p (b n) -> p b n", b=2)
        lin = W[:, 0, :]
        tt = lin[0:1, 0:6 * NT].rearrange("p (q t) -> p q t", q=6)

        xs = nc.dram_tensor("xs", (EMPTY + P, ROW), F32).ap()
        out = t["out"]

        x_in, small_in, late_in = [sem("x_in0"), sem("x_in1")], sem("small_in"), sem("late_in")
        adj_in = [sem(f"adj_in{i}") for i in range(T)]
        w_in = [sem("w1_in"), sem("w2_in")]
        const_chain, consts = sem("const_chain"), sem("consts")
        dve_chain = sem("dve_chain")
        veps_ready, rstd_ready = sem("veps_ready"), sem("rstd_ready")
        xn_ready, xnT_psum, xnT_ready = sem("xn_ready"), sem("xnT_psum"), sem("xnT_ready")
        Y_psum, Y_ready = sem("Y_psum"), sem("Y_ready")
        red_ready, rowsum_ready = sem("red_ready"), sem("rowsum_ready")
        deg_ready, deg_pow, dinv_ready = sem("deg_ready"), sem("deg_pow"), sem("dinv_ready")
        agg_ready, lin_done, x1_ready, x1_stored = (
            sem("agg_ready"), sem("lin_done"), sem("x1_ready"), [sem("x1_stored0"), sem("x1_stored1")])
        veps2_ready, rstd2_ready = sem("veps2_ready"), sem("rstd2_ready")
        logits_psum, logits_read = sem("logits_psum"), sem("logits_read")
        cum_ready, rank_psum, rank_read = sem("cum_ready"), sem("rank_psum"), sem("rank_read")
        negm_ready, exp_ready = sem("negm_ready"), sem("exp_ready")
        row_hi, slot_ready, scattered = sem("row_hi"), sem("slot_ready"), sem("scattered")
        squares, norm_psum, norm_sum = sem("squares"), sem("norm_psum"), sem("norm_sum")
        scale_ready, hi_ready, lo_ready = sem("scale_ready"), sem("hi_ready"), sem("lo_ready")
        count_psum, tables, pads_in = sem("count_psum"), sem("tables"), sem("pads_in")
        xrow_in = [sem(f"xrow_in{j}") for j in range(U)]
        xT_psum, xT_ready = sem("xT_psum"), sem("xT_ready")
        h_psum, g_ready, h_hi, h_split = sem("h_psum"), sem("g_ready"), sem("h_hi"), sem("h_split")
        y_psum, yb_ready, y_half, y_ready = (
            sem("y_psum"), sem("yb_ready"), sem("y_half"), sem("y_ready"))
        added = sem("added")
        pool_step = sem("pool_step")
        act_step, dve_step = sem("act_step"), sem("dve_step")

        block = ctx.enter_context(nc.Block())

        def tiles(body):
            def run(eng):
                for j in range(U):
                    body(0, j)
                with eng.Fori(1, LOOPS) as u:
                    for j in range(U):
                        body(u, j)
                for j in range(NT - U * LOOPS):
                    body(LOOPS, j)
            return run

        def later(u, j, n):
            u, j = u + (j + n) // U, (j + n) % U
            if isinstance(u, int) and U * u + j >= NT:
                return None
            return u, j

        @block.sync
        def _(sp):
            for c in range(2):
                sp.dma_start(x_all[:, c * T // 2:(c + 1) * T // 2, :],
                             t["x"][:, c * T // 2:(c + 1) * T // 2, :]).then_inc(x_in[c], 16)
            for i in range(T):
                sp.dma_start(arena[:, i * N:(i + 1) * N], t["adjT"][i]).then_inc(adj_in[i], 16)
            sp.wait_ge(consts, 1)
            sp.dma_start(xs[EMPTY:EMPTY + P, :], pad[:, :]).then_inc(pads_in, 16)
            sp.dma_start(out[N:N + P, :], pad[:, 0:D]).then_inc(pads_in, 16)

            def load_expert(n):
                for q, src in enumerate(("w1", "w2")):
                    if n:
                        sp.wait_ge(lo_ready, 2 * n - 1 + q)
                    sp.dma_start(stage[:, q, :], t[src][PREP[n]]).then_inc(w_in[q], 16)

            load_expert(0)
            for s in range(T):
                sp.wait_ge(x1_ready, s + 1)
                i = ORDER[s]
                sp.dma_start(out[i * P:(i + 1) * P, :], x1[:, s % 2, :])\
                  .then_inc(x1_stored[s % 2], 16)
                if s % 2 == 0 and 2 <= s:
                    load_expert(s // 2)
            sp.wait_ge(tables, 1)
            for e in range(E):
                r = sp.value_load(ptab[0:1, e:e + 1], min_val=0, max_val=EMPTY - P)
                sp.dma_start(xs[bass.ds(r, P), :], pad[:, :]).then_inc(pads_in, 16)
            sp.wait_ge(pads_in, 16 * (E + 2))
            sp.wait_ge(scattered, 16 * TOPK * T)
            sp.wait_ge(agg_ready, T)

            def load_rows(u, j):
                if not (isinstance(u, int) and u == 0):
                    sp.wait_ge(added, (u - 1) * U * 16 + (j + 1) * 16)
                r = sp.value_load(rtab[0:1, bass.ds(u * U + j, 1)], min_val=0, max_val=EMPTY)
                sp.dma_start(xrow[:, j, :], xs[bass.ds(r, P), :]).then_inc(xrow_in[j], 16)

            tiles(load_rows)(sp)

        @block.gpsimd
        def _(pool):
            n = [0]

            def link(ins):
                n[0] += 1
                ins.then_inc(const_chain, 1)
                pool.wait_ge(const_chain, n[0])

            pool.memset(identf[:, :], 0.0)
            pool.memset(identh[:, :], 0.0)
            pool.memset(onesf[:, :], 1.0)
            pool.memset(onesb[:, :], 1.0)
            pool.memset(before[:, :], 0.0)
            pool.memset(halves[:, :], -0.5)
            pool.memset(cum[:, 0, :], 0.0)
            link(pool.memset(pad[:, :], 0.0))
            for m in (identf, identh):
                pool.affine_select(out=m[:, :], in_=m[:, :], compare_op=ALU.not_equal, fill=1.0,
                                   base=0, pattern=[[-1, P]], channel_multiplier=1)
            pool.affine_select(out=before[:, :], in_=before[:, :], compare_op=ALU.is_ge, fill=1.0,
                               base=0, pattern=[[-1, P]], channel_multiplier=1)

            def iota(o, pattern, b, m):
                return pool.iota(o, pattern=pattern, base=b, channel_multiplier=m,
                                 allow_small_or_imprecise_dtypes=True)

            iota(iota8[:, :], [[1, E]], 0, 0)
            iota(eoff[:, :], [[REGION, E]], 0, 0)
            iota(tokid[:, :], [[P, T]], 0, 1)
            iota(iotat[:, :], [[1, NT]], 0, 0)
            iota(pad[:, IDCOL:IDCOL + 1], [[0, 1]], N, 1).then_inc(consts, 1)

            def power(o, v):
                return pool.tensor_tensor(o, v, halves[:, 0:v.shape[1]], ALU.pow)

            pool.wait_ge(consts, 1)
            pool.wait_ge(veps_ready, 1)
            power(rstd[:, :], veps[:, :]).then_inc(rstd_ready, 1)
            for i in range(T):
                pool.wait_ge(deg_ready, i + 1)
                power(dpow[:, i:i + 1], dmax[:, i:i + 1]).then_inc(deg_pow, 1)
            for s in range(T + 2):
                if s < T:
                    pool.wait_ge(veps2_ready, s + 1)
                    power(rstd2[:, s % 2, :], veps2[:, s % 2, :]).then_inc(rstd2_ready, 1)
                if s >= 2:
                    pool.wait_ge(slot_ready, s - 1)
                    b = (s - 2) % RB
                    for k in range(TOPK):
                        pool.indirect_dma_start(
                            xs[:, :], bass.IndirectOffsetOnAxis(ap=slot[:, b, k:k + 1], axis=0),
                            row[:, b, :], None).then_inc(scattered, 16)

            for b in range(2):
                pool.wait_ge(x1_stored[b], 16 * T // 2)
            pool.wait_ge(pads_in, 16 * (E + 2))

            def add_rows(u, j):
                first = isinstance(u, int) and u == 0 and j == 0
                if not first:
                    pool.wait_ge(added, (u * U + j) * 16)
                    pool.sem_inc(pool_step, 1)
                pool.wait_ge(y_ready, u * U + j + 1)
                pool.sem_inc(pool_step, 1)
                pool.indirect_dma_start(
                    out[:, :], bass.IndirectOffsetOnAxis(ap=idu[:, j, :], axis=0),
                    yout[:, j % 2, :], None, compute_op=ALU.add).then_inc(added, 16)

            tiles(add_rows)(pool)
            pool.wait_ge(added, 16 * NT)

        @block.scalar
        def _(act):
            for dst, src in ((W, "W"), (gw, "gate_w"), (b1, "b1")):
                act.dma_start(dst[:, :, :], t[src]).then_inc(small_in, 16)
            for dst, src in ((gb, "gate_b"), (gnnb, "gnn_b")):
                act.dma_start(dst[:, :], t[src]).then_inc(small_in, 16)

            def copy_xnT(n):
                act.wait_ge(xnT_psum, n + 1)
                if n >= 2:
                    if n - 2 < T:
                        act.wait_ge(Y_psum, n - 1)
                    else:
                        act.wait_ge(logits_psum, n - T - 1)
                act.activation(xnT[:, n % 2, :], turned(n % 2), ACT.Copy).then_inc(xnT_ready, 1)

            def copy_Y(i):
                act.wait_ge(Y_psum, i + 1)
                act.wait_ge(dinv_ready, i + 1)
                act.activation(Y[:, i, :], psum_Y(i % 2), ACT.Copy, scale=dinv[:, i:i + 1])\
                   .then_inc(Y_ready, 1)

            for i in range(T + 2):
                if i < T:
                    copy_xnT(i)
                if i >= 2:
                    copy_Y(i - 2)
                if i == T // 2:
                    act.dma_start(b2r[:, :, :], t["b2"]).then_inc(late_in, 16)

            def square_sums(n):
                if n == 0:
                    act.wait_ge(small_in, 16 * 5)
                for q in range(2):
                    act.wait_ge(w_in[q], 16 * (n + 1))
                    if n or q:
                        act.wait_ge(squares, 3 * n + q)
                    act.activation(junk, stage[:, q, :], ACT.Square,
                                   accum_out=ss[:, n, q:q + 1]).then_inc(squares, 1)
                act.wait_ge(squares, 3 * n + 2)
                act.activation(junk[:, 0:HT], b1[:, PREP[n], :], ACT.Square,
                               accum_out=ss[:, n, 2:3]).then_inc(squares, 1)

            def hi_parts(n, need):
                e = PREP[n]
                act.wait_ge(scale_ready, n + 1)
                act.wait_ge(agg_ready, need)
                act.activation(w1v[:, e, 0:WCOLS], stage[:, 0, :], ACT.Copy,
                               scale=sc[:, e, 0:1].bitcast(F32)).then_inc(hi_ready, 1)
                act.activation(w2v[:, e, :].rearrange("p (h q d) -> p h q d", q=2, d=D)[:, :, 0, :],
                               stage[:, 1, :].rearrange("p (h d) -> p h d", d=D), ACT.Copy,
                               scale=sc[:, e, 1:2].bitcast(F32)).then_inc(hi_ready, 1)

            square_sums(0)
            for s in range(T + 2):
                if 1 <= s <= T:
                    copy_xnT(T + s - 1)
                    b = (s - 1) % 2
                    act.wait_ge(negm_ready, s)
                    act.activation(ex[:, b, :], lg[:, b, :], ACT.Exp, bias=negm[:, b, :],
                                   accum_out=sumex[:, b, :]).then_inc(exp_ready, 1)
                if s % 2 == 0 and s >= 2:
                    hi_parts(s // 2 - 1, min(s + 1, T))
                if s % 2 and 3 <= s < T:
                    square_sums(s // 2)

            def copy_xT(u, j):
                act.wait_ge(xT_psum, u * U + j + 1)
                act.sem_inc(act_step, 1)
                if not (isinstance(u, int) and u * U + j < 2):
                    act.wait_ge(h_psum, HT // 2 * (u * U + j - 1))
                    act.sem_inc(act_step, 1)
                act.activation(xT[:, j % 2, :], PS[:, 6 + j % 2, 0:D].bitcast(F16), ACT.Copy)\
                   .then_inc(xT_ready, 1)

            def gelus(u, j):
                tau = u * U + j
                e = act.value_load(etab[0:1, bass.ds(tau, 1)], min_val=0, max_val=E - 1)
                for h in range(HT):
                    if h % 2 == 0:
                        act.wait_ge(h_psum, HT // 2 * tau + h // 2 + 1)
                        act.sem_inc(act_step, 1)
                    if h == 0 and not (isinstance(u, int) and tau < 2):
                        act.wait_ge(h_split, 2 * tau - 2)
                        act.sem_inc(act_step, 1)
                    act.activation(
                        g[:, j % 2, h * P:(h + 1) * P],
                        psum_h(h), ACT.Gelu,
                        bias=b1[:, bass.ds(e, 1), h:h + 1].rearrange("p a b -> p (a b)"),
                        scale=inv1[:, bass.ds(e, 1)]).then_inc(g_ready, 1)

            act.wait_ge(tables, 1)
            copy_xT(0, 0)
            copy_xT(0, 1)
            gelus(0, 0)

            def body(u, j):
                if nxt := later(u, j, 1):
                    gelus(*nxt)
                if nxt := later(u, j, 2):
                    copy_xT(*nxt)

            tiles(body)(act)

        @block.vector
        def _(dve):
            n = [0]

            def link(ins):
                n[0] += 1
                ins.then_inc(dve_chain, 1)
                dve.wait_ge(dve_chain, n[0])

            for i in range(T):
                if i % (T // 2) == 0:
                    dve.wait_ge(x_in[i // (T // 2)], 16)
                last = dve.bn_stats(stats[:, i, :], x_all[:, i, :])
            link(last)
            for i in range(T):
                last = dve.bn_aggr(mv[:, i, :], stats[:, i, :])
            link(last)
            dve.tensor_scalar(veps[:, :], mv[:, :, 1], EPS, None, ALU.add).then_inc(veps_ready, 1)
            dve.wait_ge(rstd_ready, 1)

            def degree(i):
                dve.wait_ge(rowsum_ready, i + 1)
                dve.tensor_copy(deg[:, i:i + 1], psum_sum(i))
                dve.tensor_scalar(dmax[:, i:i + 1], psum_sum(i), 2.0 ** -126, None,
                                  ALU.max).then_inc(deg_ready, 1)

            def inverse_root(i):
                dve.wait_ge(deg_pow, i + 1)
                dve.scalar_tensor_tensor(dinv[:, i:i + 1], deg[:, i:i + 1], 0.0,
                                         dpow[:, i:i + 1], ALU.is_gt, ALU.mult)\
                   .then_inc(dinv_ready, 1)

            for i in range(T + 2):
                if i < T:
                    if i >= 2:
                        dve.wait_ge(xnT_psum, i - 1)
                    dve.tensor_scalar(xn[:, i % 2, :], x_all[:, i, :], mv[:, i, 0:1],
                                      rstd[:, i:i + 1], ALU.subtract, ALU.mult)\
                       .then_inc(xn_ready, 1)
                    dve.wait_ge(adj_in[i], 16)
                    if i >= 2:
                        dve.wait_ge(rowsum_ready, i - 1)
                    dve.tensor_reduce(
                        red[:, i % 2, :],
                        arena[:, i * N:(i + 1) * N].rearrange("p (k c) -> p c k", k=T),
                        AX.X, ALU.add).then_inc(red_ready, 1)
                if 1 <= i <= T:
                    degree(i - 1)
                if i >= 2:
                    inverse_root(i - 2)

            dve.wait_ge(small_in, 16 * 5)

            def new_x(s):
                i, b = ORDER[s], s % 2
                dve.wait_ge(agg_ready, s + 1)
                if s == 0:
                    dve.wait_ge(dinv_ready, T)
                dve.scalar_tensor_tensor(lin, region(s), dinv[:, i:i + 1], gnnb[:, :],
                                         ALU.mult, ALU.add).then_inc(lin_done, 1)
                dve.wait_ge(lin_done, s + 1)
                if s >= 2:
                    dve.wait_ge(x1_stored[b], 16 * (s // 2))
                dve.scalar_tensor_tensor(x1[:, b, :], lin, 0.0, x_all[:, i, :],
                                         ALU.max, ALU.add).then_inc(x1_ready, 1)
                dve.wait_ge(x1_ready, s + 1)
                link(dve.bn_stats(stats2[:, b, :], x1[:, b, :]))
                link(dve.bn_aggr(mv2[:, b, :], stats2[:, b, :]))
                dve.tensor_scalar(veps2[:, b, :], mv2[:, b, 1:2], EPS, None, ALU.add)\
                   .then_inc(veps2_ready, 1)

            def normalise(s):
                b = s % 2
                dve.wait_ge(rstd2_ready, s + 1)
                dve.wait_ge(xnT_psum, T + s - 1)
                dve.tensor_scalar(xn[:, b, :], x1[:, b, :], mv2[:, b, 0:1], rstd2[:, b, :],
                                  ALU.subtract, ALU.mult).then_inc(xn_ready, 1)
                dve.wait_ge(xn_ready, T + s + 1)
                if s >= RB:
                    dve.wait_ge(scattered, 16 * TOPK * (s - RB + 1))
                words = row[:, s % RB, 0:D].bitcast(F16)
                dve.tensor_scalar(words[:, 0:D], xn[:, b, :], XSCALE, None, ALU.mult)\
                   .then_inc(row_hi, 1)
                dve.wait_ge(row_hi, s + 1)
                dve.scalar_tensor_tensor(words[:, D:2 * D], xn[:, b, :], XSCALE, words[:, 0:D],
                                         ALU.mult, ALU.subtract)
                dve.tensor_copy(row[:, s % RB, IDCOL:IDCOL + 1], tokid[:, ORDER[s]:ORDER[s] + 1])

            def choose(s):
                b = s % 2
                dve.wait_ge(logits_psum, s + 1)
                dve.tensor_tensor(lg[:, b, :], psum_logits, gb[:, :], ALU.add)\
                   .then_inc(logits_read, 1)
                dve.wait_ge(logits_read, s + 1)
                link(dve.max(top8[:, b, :], lg[:, b, :]))
                dve.tensor_scalar(negm[:, b, :], top8[:, b, 0:1], -1.0, None, ALU.mult)\
                   .then_inc(negm_ready, 1)
                link(dve.max_index(idx8[:, :], top8[:, b, :], lg[:, b, :]))
                link(dve.tensor_copy(idxf[:, :], idx8[:, 0:TOPK]))
                for k in range(TOPK):
                    last = dve.tensor_scalar(oh[:, b, k, :], iota8[:, :], idxf[:, k:k + 1], None,
                                             ALU.is_equal)
                link(last)
                link(dve.tensor_tensor(mask[:, b, :], oh[:, b, 0, :], oh[:, b, 1, :], ALU.add))
                dve.tensor_tensor(cum[:, s + 1, :], cum[:, s, :], mask[:, b, :], ALU.add)\
                   .then_inc(cum_ready, 1)

            def gates(s):
                b = s % 2
                dve.wait_ge(exp_ready, s + 1)
                link(dve.reciprocal(rsum[:, b, :], sumex[:, b, :]))
                dve.scalar_tensor_tensor(row[:, s % RB, GATE0:GATE0 + E], ex[:, b, :],
                                         rsum[:, b, :], mask[:, b, :], ALU.mult, ALU.mult)

            def slots(s):
                b = s % 2
                dve.wait_ge(rank_psum, s + 1)
                dve.tensor_tensor(base[:, :], psum_rank, eoff[:, :], ALU.add)\
                   .then_inc(rank_read, 1)
                dve.wait_ge(rank_read, s + 1)
                for k in range(TOPK):
                    last = dve.tensor_tensor_reduce(tmp8[:, k, :], oh[:, b, k, :], base[:, :],
                                                    1.0, 0.0, ALU.mult, ALU.add, slotf[:, k:k + 1])
                link(last)
                dve.tensor_copy(slot[:, s % RB, :], slotf[:, :]).then_inc(slot_ready, 1)

            def scales(n):
                e = PREP[n]
                dve.wait_ge(norm_psum, n + 1)
                link(dve.tensor_scalar(ntmp[:, :], psum_norm[:, 2:3], 2.0, None, ALU.mult))
                dve.tensor_copy(nsum[:, 0:2], psum_norm[:, 0:2])
                dve.scalar_tensor_tensor(nsum[:, 2:3], psum_norm[:, 0:1], 2.0 * D, ntmp[:, :],
                                         ALU.mult, ALU.add).then_inc(norm_sum, 1)
                dve.wait_ge(norm_sum, n + 1)
                link(dve.tensor_scalar(mexp[:, :], nsum[:, :].bitcast(I32), 24, None,
                                       ALU.logical_shift_right))
                dve.tensor_scalar(sc[:, e, :], mexp[:, :], -float(EXPO_UNIT),
                                  204.0 * EXPO_UNIT, ALU.mult, ALU.add).then_inc(scale_ready, 1)
                link(dve.tensor_scalar(inv[:, :], mexp[:, :], float(EXPO_UNIT),
                                       50.0 * EXPO_UNIT, ALU.mult, ALU.add))
                invf = inv[:, :].bitcast(F32)
                dve.tensor_scalar(inv1[:, e:e + 1], invf[:, 0:1], 1.0 / XSCALE, None, ALU.mult)
                dve.tensor_tensor(inv2[:, e:e + 1], invf[:, 1:2], invf[:, 2:3], ALU.mult)

            def lo_parts(n):
                e = PREP[n]
                w2 = w2v[:, e, :].rearrange("p (h q d) -> p h q d", q=2, d=D)
                outs = w1v[:, e, WCOLS:2 * WCOLS], w2[:, :, 1, :]
                his = w1v[:, e, 0:WCOLS], w2[:, :, 0, :]
                src = stage[:, 0, :], stage[:, 1, :].rearrange("p (h d) -> p h d", d=D)
                for q in range(2):
                    dve.wait_ge(hi_ready, 2 * n + q + 1)
                    dve.scalar_tensor_tensor(outs[q], src[q], sc[:, e, q:q + 1].bitcast(F32),
                                             his[q], ALU.mult, ALU.subtract).then_inc(lo_ready, 1)

            for s in range(T + 2):
                if s < T:
                    new_x(s)
                if 1 <= s <= T:
                    choose(s - 1)
                if s % 2 == 0 and s >= 2:
                    scales(s // 2 - 1)
                if s < T:
                    normalise(s)
                if 1 <= s <= T:
                    gates(s - 1)
                if s >= 2:
                    slots(s - 2)
                if s % 2 == 0 and s >= 2:
                    lo_parts(s // 2 - 1)

            dve.wait_ge(count_psum, 1)
            dve.tensor_scalar(tli[:, 0, :], psum_count, float(P - 1), None, ALU.add)
            link(dve.tensor_tensor(ptab[0:1, :], psum_count[0:1, :], eoff[0:1, :], ALU.add))
            link(dve.tensor_scalar(tli[:, 1, :], tli[:, 0, :], P.bit_length() - 1, None,
                                   ALU.logical_shift_right))
            link(dve.tensor_copy(tl[:, 0, :], tli[:, 1, :]))
            link(dve.tensor_tensor_scan(tl[:, 1, :], onesf[:, 0:E], tl[:, 0, :], 0.0,
                                        ALU.mult, ALU.add))
            for e in range(E):
                dve.tensor_scalar(cmp[:, 0, e, :], iotat[0:1, :], tl[0:1, 1, e:e + 1], None,
                                  ALU.is_ge)
                last = dve.tensor_scalar(cmp[:, 1, e, :], iotat[0:1, :], tl[0:1, 1, e:e + 1],
                                         tl[0:1, 0, e:e + 1], ALU.is_ge, ALU.mult)
            link(last)
            for q in range(2):
                last = dve.tensor_reduce(tt[:, q, :], cmp[:, q, :, :].rearrange("p e t -> p t e"),
                                         AX.X, ALU.add)
            link(last)
            link(dve.tensor_tensor(tt[:, 2, :], iotat[0:1, :], tt[:, 1, :], ALU.subtract))
            link(dve.tensor_scalar(tt[:, 3, :], tt[:, 2, :], float(P), None, ALU.mult))
            link(dve.scalar_tensor_tensor(tt[:, 4, :], tt[:, 0, :], float(REGION), tt[:, 3, :],
                                          ALU.mult, ALU.add))
            dve.tensor_scalar(etab[:, :], tt[:, 0, :], float(E - 1), None, ALU.min)
            dve.tensor_scalar(rtab[:, :], tt[:, 4, :], float(EMPTY), None, ALU.min)\
               .then_inc(tables, 1)

            dve.wait_ge(tables, 1)
            def split(u, j, halves_):
                tau = u * U + j
                e = dve.value_load(etab[0:1, bass.ds(tau, 1)], min_val=0, max_val=E - 1)
                s = sc[:, :, :].bitcast(F32)[:, bass.ds(e, 1), 2:3].rearrange("p a b -> p (a b)")
                half = H // 2
                for q in halves_:
                    cols = slice(q * half, (q + 1) * half)
                    dve.wait_ge(g_ready, HT * tau + (q + 1) * HT // 2)
                    dve.sem_inc(dve_step, 1)
                    if q == 0 and not (isinstance(u, int) and tau < 2):
                        dve.wait_ge(y_psum, tau - 1)
                        dve.sem_inc(dve_step, 1)
                    dve.tensor_scalar(hs[:, j % 2, 0, cols], g[:, j % 2, cols], s, None,
                                      ALU.mult).then_inc(h_hi, 1)
                    dve.wait_ge(h_hi, 2 * tau + q + 1)
                    dve.sem_inc(dve_step, 1)
                    dve.scalar_tensor_tensor(hs[:, j % 2, 1, cols], g[:, j % 2, cols], s,
                                             hs[:, j % 2, 0, cols], ALU.mult, ALU.subtract)\
                       .then_inc(h_split, 1)

            def result(u, j):
                tau = u * U + j
                e = dve.value_load(etab[0:1, bass.ds(tau, 1)], min_val=0, max_val=E - 1)
                gate = xrow[:, j, GATE0:GATE0 + E][:, bass.ds(e, 1)]
                dve.wait_ge(xrow_in[j], (u + 1) * 16)
                dve.sem_inc(dve_step, 1)
                if not (isinstance(u, int) and tau < 2):
                    dve.wait_ge(added, (tau - 1) * 16)
                    dve.sem_inc(dve_step, 1)
                dve.tensor_copy(idu[:, j, :], xrow[:, j, IDCOL:IDCOL + 1])
                dve.tensor_tensor(gs[:, j % 2, :], gate, inv2[:, bass.ds(e, 1)], ALU.mult)
                dve.tensor_scalar(yb[:, j % 2, :],
                                  b2r[:, bass.ds(e, 1), :].rearrange("p a b -> p (a b)"),
                                  gate, None, ALU.mult).then_inc(yb_ready, 1)

            def add_up(u, j):
                tau = u * U + j
                o, p = yout[:, j % 2, :], PS[:, 4 + j % 2, :]
                dve.wait_ge(yb_ready, tau + 1)
                dve.sem_inc(dve_step, 1)
                dve.wait_ge(y_psum, tau + 1)
                dve.sem_inc(dve_step, 1)
                dve.scalar_tensor_tensor(o, p[:, 0:D], gs[:, j % 2, :], yb[:, j % 2, :],
                                         ALU.mult, ALU.add).then_inc(y_half, 1)
                dve.wait_ge(y_half, tau + 1)
                dve.sem_inc(dve_step, 1)
                dve.scalar_tensor_tensor(o, p[:, D:2 * D], gs[:, j % 2, :], o,
                                         ALU.mult, ALU.add).then_inc(y_ready, 1)

            dve.wait_ge(late_in, 16)
            split(0, 0, (0, 1))

            def body(u, j):
                result(u, j)
                nxt = later(u, j, 1)
                if nxt:
                    split(*nxt, (0,))
                add_up(u, j)
                if nxt:
                    split(*nxt, (1,))

            tiles(body)(dve)

        @block.tensor
        def _(pe):
            def transposes(n):
                pe.wait_ge(xn_ready, n + 1)
                if n >= 2:
                    pe.wait_ge(xnT_ready, n - 1)
                for k in range(KD):
                    last = pe.transpose(turned(n % 2)[:, k * P:(k + 1) * P],
                                        xn[:, n % 2, k * P:(k + 1) * P], identf[:, :])
                last.then_inc(xnT_psum, 1)

            def product_W(i):
                pe.wait_ge(xnT_ready, i + 1)
                if i >= 2:
                    pe.wait_ge(Y_ready, i - 1)
                for k in range(KD):
                    last = pe.matmul(psum_Y(i % 2), xnT[:, i % 2, k * P:(k + 1) * P],
                                     W[:, k, :], start=(k == 0), stop=(k == KD - 1))
                last.then_inc(Y_psum, 1)

            def rowsum(i):
                pe.wait_ge(red_ready, i + 1)
                if i >= 2:
                    pe.wait_ge(deg_ready, i - 1)
                pe.matmul(psum_sum(i), red[:, i % 2, :], onesf[:, 0:1], start=True,
                          stop=True).then_inc(rowsum_ready, 1)

            half = T // 2

            def adj_product(s, ks, first=False):
                i, r = ORDER[s], region(s)
                before_it = [p for p in range(s) if BANKS[p] == BANKS[s]]
                if before_it and not first:
                    pe.wait_ge(lin_done, before_it[-1] + 1)
                for k in ks:
                    if s == 0 or first:
                        pe.wait_ge(Y_ready, k + 1)
                    c = i * N + k * P
                    last = pe.matmul(r, arena[:, c:c + P], Y[:, k, :],
                                     start=(k == 0 and not (i < EARLY and i % 2)),
                                     stop=(k == T - 1), skip_group_check=True)
                if ks[-1] == T - 1:
                    last.then_inc(agg_ready, 1)

            def logits(s):
                pe.wait_ge(xnT_ready, T + s + 1)
                if s:
                    pe.wait_ge(logits_read, s)
                for k in range(KD):
                    last = pe.matmul(psum_logits, xnT[:, s % 2, k * P:(k + 1) * P], gw[:, k, :],
                                     start=(k == 0), stop=(k == KD - 1))
                last.then_inc(logits_psum, 1)

            def ranks(s):
                pe.wait_ge(cum_ready, s + 1)
                if s:
                    pe.wait_ge(rank_read, s)
                pe.matmul(psum_rank, before[:, :], mask[:, s % 2, :], start=True, stop=False)
                pe.matmul(psum_rank, onesb[:, :], cum[:, s, :], start=False, stop=True)\
                  .then_inc(rank_psum, 1)

            def norms(n):
                pe.wait_ge(squares, 3 * n + 3)
                if n:
                    pe.wait_ge(norm_sum, n)
                pe.matmul(psum_norm, onesf[:, :], ss[:, n, :], start=True, stop=True)\
                  .then_inc(norm_psum, 1)

            pe.wait_ge(consts, 1)
            pe.wait_ge(small_in, 16 * 5)
            early = [(ORDER.index(i), range(a, a + half // 2))
                     for i in range(EARLY) for a in (0, half // 2)]
            for i in range(T + 1):
                if i < T:
                    transposes(i)
                if i:
                    product_W(i - 1)
                if i < T:
                    rowsum(i)
                if i > half:
                    adj_product(*early[i - half - 1], first=True)

            for s in range(T + 2):
                if s < T:
                    done = half if ORDER[s] < EARLY else 0
                    cuts = [done, done + (3 if not done else 1), done + (T - done) // 2, T]
                    adj_product(s, range(cuts[0], cuts[1]))
                if s % 2 and s >= 3:
                    norms((s - 3) // 2)
                if s < T:
                    adj_product(s, range(cuts[1], cuts[2]))
                if 1 <= s <= T:
                    transposes(T + s - 1)
                if s >= 2:
                    ranks(s - 2)
                if s < T:
                    adj_product(s, range(cuts[2], T))
                if 1 <= s <= T:
                    logits(s - 1)
            pe.wait_ge(logits_read, T)
            pe.matmul(psum_count, onesb[:, :], cum[:, T, :], start=True, stop=True)\
              .then_inc(count_psum, 1)

            pe.wait_ge(rank_read, T)
            pe.wait_ge(lo_ready, 2 * E)

            def expert(u, j):
                return pe.value_load(etab[0:1, bass.ds(u * U + j, 1)], min_val=0, max_val=E - 1)

            def w1_at(e, q, c):
                c += q * WCOLS
                return w1v[:, bass.ds(e, 1), c:c + P].rearrange("p a b -> p (a b)")

            def w2_at(e, h):
                return w2v[:, bass.ds(e, 1), 2 * h * D:2 * (h + 1) * D]\
                    .rearrange("p a b -> p (a b)")

            def turn_rows(u, j):
                pe.wait_ge(xrow_in[j], (u + 1) * 16)
                if not (isinstance(u, int) and u * U + j < 2):
                    pe.wait_ge(xT_ready, u * U + j - 1)
                words = xrow[:, j, 0:D].bitcast(F16)
                for k in range(2 * KD):
                    last = pe.transpose(PS[:, 6 + j % 2, 0:D].bitcast(F16)[:, k * P:(k + 1) * P],
                                        words[:, k * P:(k + 1) * P], identh[:, :])
                last.then_inc(xT_psum, 1)

            def up(e, u, j, h):
                tau = u * U + j
                if h == 0:
                    pe.wait_ge(xT_ready, tau + 1)
                if h % 2 == 0 and not (isinstance(u, int) and tau == 0):
                    pe.wait_ge(g_ready, HT * (tau - 1) + h + 2)
                o = psum_h(h)
                for k in range(KD):
                    c = k * H + h * P
                    x_hi = xT[:, j % 2, k * P:(k + 1) * P]
                    x_lo = xT[:, j % 2, (KD + k) * P:(KD + k + 1) * P]
                    hi = w1_at(e, 0, c)
                    pe.matmul(o, hi, x_hi, start=(k == 0), stop=False)
                    pe.matmul(o, hi, x_lo, start=False, stop=False)
                    last = pe.matmul(o, w1_at(e, 1, c), x_hi, start=False, stop=(k == KD - 1))
                if h % 2:
                    last.then_inc(h_psum, 1)

            def down(e, u, j, h):
                tau = u * U + j
                if h == 0 and not (isinstance(u, int) and tau < 2):
                    pe.wait_ge(y_ready, tau - 1)
                if h % 4 == 0:
                    pe.wait_ge(h_split, 2 * tau + h // 4 + 1)
                o, w = PS[:, 4 + j % 2, :], w2_at(e, h)
                cols = slice(h * P, (h + 1) * P)
                pe.matmul(o, hs[:, j % 2, 0, cols], w, start=(h == 0), stop=False)
                last = pe.matmul(o[:, 0:D], hs[:, j % 2, 1, cols], w[:, 0:D], start=False,
                                 stop=(h == HT - 1))
                if h == HT - 1:
                    last.then_inc(y_psum, 1)

            pe.wait_ge(tables, 1)
            turn_rows(0, 0)
            turn_rows(0, 1)
            e0 = expert(0, 0)
            for h in range(HT):
                up(e0, 0, 0, h)
            known = [None, e0]

            def body(u, j):
                if j == 0:
                    known[1] = expert(u, j)
                known[0] = known[1]
                nxt, after = later(u, j, 1), later(u, j, 2)
                if nxt:
                    known[1] = expert(*nxt)
                for h in range(HT):
                    if nxt:
                        up(known[1], *nxt, h)
                    down(known[0], u, j, h)
                    if h == HT // 2 - 1 and after:
                        turn_rows(*after)

            tiles(body)(pe)


def kernel(**inputs):
    import numpy as np
    import concourse.bacc as bacc
    from concourse.bass_utils import run_bass_kernel_spmd

    def rows(a, p=P):
        return np.broadcast_to(np.asarray(a).reshape(1, -1), (p, np.asarray(a).size))

    i = {k: np.asarray(v) for k, v in inputs.items()}
    arrays = {
        "x": i["x"].reshape(T, P, D).transpose(1, 0, 2),
        "adjT": i["adj"].reshape(T, P, T, P).transpose(0, 3, 2, 1).reshape(T, P, N),
        "W": i["L0_gnn_W"].reshape(KD, P, D).transpose(1, 0, 2),
        "gnn_b": rows(i["L0_gnn_b"]),
        "gate_w": i["L0_ffn_gate_w"].reshape(KD, P, E).transpose(1, 0, 2),
        "gate_b": rows(i["L0_ffn_gate_b"]),
        "w1": i["L0_ffn_w1"].reshape(E, KD, P, H).transpose(0, 2, 1, 3).reshape(E, P, WCOLS),
        "b1": i["L0_ffn_b1"].reshape(E, HT, P).transpose(2, 0, 1),
        "w2": i["L0_ffn_w2"].reshape(E, HT, P, D).transpose(0, 2, 1, 3).reshape(E, P, WCOLS),
        "b2": rows(i["L0_ffn_b2"]).reshape(P, E, D),
    }
    arrays = {f"{k}_in": np.ascontiguousarray(v) for k, v in arrays.items()}
    nc = bacc.Bacc("TRN2", target_bir_lowering=False, num_devices=1)
    t = {k[:-3]: nc.dram_tensor(k, v.shape, F32, kind="ExternalInput").ap()
         for k, v in arrays.items()}
    t["out"] = nc.dram_tensor("y_out", (N + P, D), F32, kind="ExternalOutput").ap()
    build(nc, t)
    r = run_bass_kernel_spmd(nc, [arrays], core_ids=[0])
    return r.results[0]["y_out"][:N]
```

```python
from contextlib import ExitStack

import concourse.bass as bass
from concourse import mybir

F32, F16, BF16 = mybir.dt.float32, mybir.dt.float16, mybir.dt.bfloat16
I32, U32 = mybir.dt.int32, mybir.dt.uint32
ACT, ALU, AX = mybir.ActivationFunctionType, mybir.AluOpType, mybir.AxisListType

P = 128
N, D, H, E, TOPK = 2048, 256, 1024, 8, 2
T = N // P
KD = D // P
HT = H // P
NT = TOPK * T + E - 1
REGION = N + P
EMPTY = E * REGION
ROW = D + E + 1
GATE0, IDCOL = D, D + E
EPS = 1e-5
XSCALE = 2.0 ** 11
EXPO_UNIT = 1 << 23
U = 8
EARLY, EARLY_KS = 6, 7
EARLY_ROUNDS = (range(0, 2), range(2, 6), range(6, EARLY_KS))
ORDER = [0, 6, 7, 1, 8, 2, 9, 10, 3, 11, 12, 4, 13, 5, 14, 15]
BANKS = [0, 4, 5, 0, 4, 1, 5, 4, 1, 5, 4, 7, 5, 7, 4, 5]
PREP = [3, 0, 4, 1, 5, 6, 2, 7]
XG = 4
RB = 3
LOOPS = NT // U
PACK = U // 2
WORDS = 2 * (LOOPS + 1)
NTX = (WORDS + 1) * PACK
BITS = (E - 1).bit_length()
WCOLS = KD * H


def build(nc, t):
    ctx = ExitStack()
    with ctx:
        def sb(name, shape, dt=F32):
            return ctx.enter_context(nc.sbuf_tensor(name, shape, dt))

        def sem(name):
            return ctx.enter_context(nc.semaphore(name))

        arena = sb("arena", [P, T * N])
        Y = sb("Y", [P, T, D])
        stage = sb("stage", [P, 2, 2, WCOLS])
        b2r = sb("b2r", [P, E, D])
        gnnb = sb("gnnb", [P, D])
        W = sb("W", [P, KD, D])
        gw = sb("gw", [P, KD, E])
        gb = sb("gb", [P, E])
        b1 = sb("b1", [P, E, HT])
        xn = sb("xn", [P, 2, D])
        xnT = sb("xnT", [P, 2, D])
        nmr = sb("nmr", [P, T])
        x1 = sb("x1", [P, 2, D])
        row = sb("row", [P, RB, ROW])
        red = sb("red", [P, 2, P])
        scratch = sb("scratch", [P, WCOLS // 2])
        pad = sb("pad", [P, ROW])
        warm = sb("warm", [P, 1])
        identf = sb("identf", [P, P])
        identh = sb("identh", [P, P], F16)
        onesf = sb("onesf", [P, P])
        onesb = sb("onesb", [P, P], BF16)
        before = sb("before", [P, P], BF16)
        iota8 = sb("iota8", [P, E])
        eoff = sb("eoff", [P, E])
        tokid = sb("tokid", [P, T])
        iotat = sb("iotat", [P, NTX])
        stats = sb("stats", [P, T, 6])
        mv = sb("mv", [P, T, 2])
        veps = sb("veps", [P, T])
        rstd = sb("rstd", [P, T])
        deg = sb("deg", [P, T])
        dmax = sb("dmax", [P, T])
        dpow = sb("dpow", [P, T])
        halves = sb("halves", [P, T])
        dinv = sb("dinv", [P, T])
        stats2 = sb("stats2", [P, 2, 6])
        mv2 = sb("mv2", [P, 2, 2])
        veps2 = sb("veps2", [P, 2, 1])
        rstd2 = sb("rstd2", [P, 2, 1])
        lg = sb("lg", [P, 2, E])
        top8 = sb("top8", [P, 2, E])
        idx8 = sb("idx8", [P, E], U32)
        idxf = sb("idxf", [P, 2])
        oh = sb("oh", [P, 2, TOPK, E])
        mask = sb("mask", [P, 2, E], BF16)
        cum = sb("cum", [P, T + 1, E], BF16)
        negm = sb("negm", [P, 2, 1])
        ex = sb("ex", [P, 2, E])
        sumex = sb("sumex", [P, 2, 1])
        rsum = sb("rsum", [P, 2, 1])
        base = sb("base", [P, E])
        tmp8 = sb("tmp8", [P, TOPK, E])
        slotf = sb("slotf", [P, TOPK])
        slot = sb("slot", [P, RB, TOPK], U32)
        ss = sb("ss", [P, E, 3])
        nsum = sb("nsum", [P, 3])
        ntmp = sb("ntmp", [P, 1])
        mexp = sb("mexp", [P, 3], I32)
        inv = sb("inv", [P, 3], I32)
        sc = sb("sc", [P, E, 3], I32)
        inv1 = sb("inv1", [P, E])
        inv2 = sb("inv2", [P, E])
        tl = sb("tl", [P, 6, E])
        tli = sb("tli", [P, 2, E], I32)
        ptab = sb("ptab", [1, E], I32)
        idu = sb("idu", [P, U, 1], U32)
        gs = sb("gs", [P, 2, 1])
        PS = ctx.enter_context(nc.psum_tensor("PS", [P, 8, 512], F32))

        halfwords = arena[:, :].bitcast(F16).rearrange("p (e w n) -> p e w n", e=E, w=2)
        w1v = halfwords[:, :, 0, :]
        w2v = halfwords[:, :, 1, :]

        def region(s):
            part = ORDER[s] % 2 if ORDER[s] < EARLY else 0
            return PS[:, BANKS[s], part * D:(part + 1) * D]

        def turned(b):
            return PS[:, 2 + b, 0:D]

        def psum_Y(b):
            return PS[:, 4 + b, 0:D]

        def psum_sum(i):
            return PS[:, 6, i:i + 1]

        def psum_rank(s):
            return PS[:, 2 + s % 2, D:D + E]

        psum_logits, psum_count, psum_norm = PS[:, 6, 0:E], PS[:, 6, E:2 * E], PS[:, 6, 32:35]

        def psum_h(h):
            return PS[:, h // 2, (h % 2) * P:(h % 2 + 1) * P]

        junk = scratch[:, :].bitcast(BF16)
        cmp = scratch[0:1, 0:2 * E * NTX].rearrange("p (q e t) -> p q e t", q=2, e=E)
        xflat = stage[:, 0, :, :].rearrange("p q n -> p (q n)")
        x_all = xflat.rearrange("p (t d) -> p t d", d=D)
        yflat = Y[:, :, :].rearrange("p t d -> p (t d)")
        g = xflat[:, 0:2 * H].rearrange("p (b n) -> p b n", b=2)
        hs = xflat[:, 2 * H:4 * H].bitcast(F16).rearrange("p (b q n) -> p b q n", b=2, q=2)
        xrow = yflat[:, 0:U * ROW].rearrange("p (b n) -> p b n", b=U)
        y0 = U * ROW
        xT = yflat[:, y0:y0 + 2 * D].bitcast(F16).rearrange("p (b n) -> p b n", b=2)
        yout = yflat[:, y0 + 2 * D:y0 + 4 * D].rearrange("p (b n) -> p b n", b=2)
        yb = yflat[:, y0 + 4 * D:y0 + 6 * D].rearrange("p (b n) -> p b n", b=2)
        tables_at = y0 + 6 * D
        etab = yflat[0:1, tables_at:tables_at + NTX].bitcast(I32)
        rtab = yflat[0:1, tables_at + NTX:tables_at + 2 * NTX].bitcast(I32)
        packs = yflat[0:1, tables_at + 2 * NTX:tables_at + 2 * NTX + 4 * WORDS]
        pk = packs.rearrange("p (q n) -> p q n", q=4)
        packed = pk[:, 3, :].bitcast(I32)
        lin = W[:, 0, :]
        tt = lin[0:1, 0:5 * NTX].rearrange("p (q t) -> p q t", q=5)

        xs = nc.dram_tensor("xs", (EMPTY + P, ROW), F32).ap()
        out = t["out"]

        x_in = [sem(f"x_in{g}") for g in range(XG)]
        W_in, small_in, late_in = sem("W_in"), sem("small_in"), sem("late_in")
        again_in = [sem("again_in0"), sem("again_in1")]
        adj_in = [sem(f"adj_in{i}") for i in range(T)]
        w_in = [[sem("w1_in0"), sem("w2_in0")], [sem("w1_in1"), sem("w2_in1")]]
        const_chain, consts = sem("const_chain"), sem("consts")
        dve_chain = sem("dve_chain")
        veps_ready, rstd_ready, nmr_ready = sem("veps_ready"), sem("rstd_ready"), sem("nmr_ready")
        xn_ready, xnT_psum, xnT_ready = sem("xn_ready"), sem("xnT_psum"), sem("xnT_ready")
        Y_psum, Y_ready = sem("Y_psum"), sem("Y_ready")
        red_ready, rowsum_ready = sem("red_ready"), sem("rowsum_ready")
        deg_ready, deg_pow, dinv_ready = sem("deg_ready"), sem("deg_pow"), sem("dinv_ready")
        agg_ready, lin_done, x1_ready, x1_stored = (
            sem("agg_ready"), sem("lin_done"), sem("x1_ready"), [sem("x1_stored0"), sem("x1_stored1")])
        veps2_ready, rstd2_ready = sem("veps2_ready"), sem("rstd2_ready")
        logits_psum, logits_read = sem("logits_psum"), sem("logits_read")
        cum_ready, rank_psum, rank_read = sem("cum_ready"), sem("rank_psum"), sem("rank_read")
        negm_ready, exp_ready = sem("negm_ready"), sem("exp_ready")
        row_hi, slot_ready = sem("row_hi"), sem("slot_ready")
        scattered = [sem(f"scattered{b}") for b in range(RB)]
        squares, norm_psum, norm_sum = sem("squares"), sem("norm_psum"), sem("norm_sum")
        scale_ready, hi_ready, lo_ready = sem("scale_ready"), sem("hi_ready"), sem("lo_ready")
        rows_known = sem("rows_known")
        count_psum, ptab_ready, tables, pads_in = (
            sem("count_psum"), sem("ptab_ready"), sem("tables"), sem("pads_in"))
        xrow_in = [sem(f"xrow_in{j}") for j in range(U)]
        xT_psum, xT_ready = sem("xT_psum"), sem("xT_ready")
        h_psum, g_ready, h_hi, h_split = sem("h_psum"), sem("g_ready"), sem("h_hi"), sem("h_split")
        y_psum, yb_ready, y_half, y_ready = (
            sem("y_psum"), sem("yb_ready"), sem("y_half"), sem("y_ready"))
        added = sem("added")
        pool_step = sem("pool_step")
        act_step, dve_step = sem("act_step"), sem("dve_step")

        block = ctx.enter_context(nc.Block())

        def tiles(body):
            def run(eng):
                for j in range(U):
                    body(0, j)
                with eng.Fori(1, LOOPS) as u:
                    for j in range(U):
                        body(u, j)
                for j in range(NT - U * LOOPS):
                    body(LOOPS, j)
            return run

        def later(u, j, n):
            u, j = u + (j + n) // U, (j + n) % U
            if isinstance(u, int) and U * u + j >= NT:
                return None
            return u, j

        def pad_regions(eng, engine_type, experts):
            eng.wait_ge(ptab_ready, 1)
            _, ends = nc.values_load_multi_w_load_instructions(
                ptab[0:1, experts.start:experts.stop:experts.step], engines=[engine_type],
                min_val=0, max_val=EMPTY - P)
            for r in ends:
                eng.dma_start(xs[bass.ds(r, P), :], pad[:, :]).then_inc(pads_in, 16)

        @block.sync
        def _(sp):
            G = T // XG
            for i in range(T):
                if i % 2 == 0 and i // 2 < XG:
                    group = slice(i // 2 * G, (i // 2 + 1) * G)
                    sp.dma_start(x_all[:, group, :], t["x"][:, group, :])\
                      .then_inc(x_in[i // 2], 16)
                sp.dma_start(arena[:, i * N:(i + 1) * N], t["adjT"][i]).then_inc(adj_in[i], 16)
            sp.dma_start(b2r[:, :, :], t["b2"]).then_inc(late_in, 16)
            sp.wait_ge(consts, 1)
            sp.dma_start(xs[EMPTY:EMPTY + P, :], pad[:, :]).then_inc(pads_in, 16)
            sp.dma_start(out[N:N + P, :], pad[:, 0:D]).then_inc(pads_in, 16)

            def load_weights(n, q):
                if n == 1:
                    sp.wait_ge(xn_ready, T)
                if n >= 2:
                    sp.wait_ge(lo_ready, 2 * (n - 2) + q + 1)
                sp.dma_start(stage[:, (n + 1) % 2, q, :], t[("w1", "w2")[q]][PREP[n]])\
                  .then_inc(w_in[n % 2][q], 16)

            def load_x(s):
                sp.dma_start(x1[:, s % 2, :], t["x"][:, ORDER[s], :]).then_inc(again_in[s % 2], 16)

            load_x(0)
            load_x(1)
            for n in range(2):
                for q in range(2):
                    load_weights(n, q)
            for s in range(T):
                sp.wait_ge(x1_ready, s + 1)
                i = ORDER[s]
                sp.dma_start(out[i * P:(i + 1) * P, :], x1[:, s % 2, :])\
                  .then_inc(x1_stored[s % 2], 16)
                if s >= 1 and s + 1 < T:
                    sp.wait_ge(x1_stored[(s + 1) % 2], 16 * ((s + 1) // 2))
                    sp.wait_ge(xn_ready, T + s)
                    load_x(s + 1)
                if s >= 3 and (s + 1) // 2 < E:
                    load_weights((s + 1) // 2, (s + 1) % 2)
            pad_regions(sp, mybir.EngineType.SP, range(0, E, 2))
            sp.wait_ge(rows_known, 1)
            sp.wait_ge(pads_in, 16 * (E + 2))
            for b in range(RB):
                sp.wait_ge(scattered[b], 16 * TOPK * len(range(b, T, RB)))
            sp.wait_ge(agg_ready, T)

            def load_rows(u, j):
                if not (isinstance(u, int) and u == 0):
                    sp.wait_ge(added, (u - 1) * U * 16 + (j + 1) * 16)
                r = sp.value_load(rtab[0:1, bass.ds(u * U + j, 1)], min_val=0, max_val=EMPTY)
                sp.dma_start(xrow[:, j, :], xs[bass.ds(r, P), :]).then_inc(xrow_in[j], 16)

            tiles(load_rows)(sp)

        @block.gpsimd
        def _(pool):
            n = [0]

            def link(ins):
                n[0] += 1
                ins.then_inc(const_chain, 1)
                pool.wait_ge(const_chain, n[0])

            pool.memset(identf[:, :], 0.0)
            pool.memset(identh[:, :], 0.0)
            pool.memset(onesf[:, :], 1.0)
            pool.memset(onesb[:, :], 1.0)
            pool.memset(before[:, :], 0.0)
            pool.memset(halves[:, :], -0.5)
            pool.memset(cum[:, 0, :], 0.0)
            link(pool.memset(pad[:, :], 0.0))
            for m in (identf, identh):
                pool.affine_select(out=m[:, :], in_=m[:, :], compare_op=ALU.not_equal, fill=1.0,
                                   base=0, pattern=[[-1, P]], channel_multiplier=1)
            pool.affine_select(out=before[:, :], in_=before[:, :], compare_op=ALU.is_ge, fill=1.0,
                               base=0, pattern=[[-1, P]], channel_multiplier=1)

            def iota(o, pattern, b, m):
                return pool.iota(o, pattern=pattern, base=b, channel_multiplier=m,
                                 allow_small_or_imprecise_dtypes=True)

            iota(iota8[:, :], [[1, E]], 0, 0)
            iota(eoff[:, :], [[REGION, E]], 0, 0)
            iota(tokid[:, :], [[P, T]], 0, 1)
            iota(iotat[:, :], [[1, NTX]], 0, 0)
            iota(pad[:, IDCOL:IDCOL + 1], [[0, 1]], N, 1).then_inc(consts, 1)

            def power(o, v):
                return pool.tensor_tensor(o, v, halves[:, 0:v.shape[1]], ALU.pow)

            pool.wait_ge(consts, 1)
            G = T // XG
            for i in range(-1, T):
                if i % 2 and (i + 1) // 2 < XG:
                    g = (i + 1) // 2
                    pool.wait_ge(veps_ready, g + 1)
                    power(rstd[:, g * G:(g + 1) * G], veps[:, g * G:(g + 1) * G])\
                        .then_inc(rstd_ready, 1)
                if i < 0:
                    continue
                pool.wait_ge(deg_ready, i + 1)
                power(dpow[:, i:i + 1], dmax[:, i:i + 1]).then_inc(deg_pow, 1)
            for s in range(T + 2):
                if s < T:
                    pool.wait_ge(veps2_ready, s + 1)
                    power(rstd2[:, s % 2, :], veps2[:, s % 2, :]).then_inc(rstd2_ready, 1)
                if s >= 2:
                    pool.wait_ge(slot_ready, s - 1)
                    b = (s - 2) % RB
                    for k in range(TOPK):
                        pool.indirect_dma_start(
                            xs[:, :], bass.IndirectOffsetOnAxis(ap=slot[:, b, k:k + 1], axis=0),
                            row[:, b, :], None).then_inc(scattered[b], 16)

            for b in range(2):
                pool.wait_ge(x1_stored[b], 16 * T // 2)
            pool.wait_ge(pads_in, 16 * (E + 2))

            def add_rows(u, j):
                first = isinstance(u, int) and u == 0 and j == 0
                if not first:
                    pool.wait_ge(added, (u * U + j) * 16)
                    pool.sem_inc(pool_step, 1)
                pool.wait_ge(y_ready, u * U + j + 1)
                pool.sem_inc(pool_step, 1)
                pool.indirect_dma_start(
                    out[:, :], bass.IndirectOffsetOnAxis(ap=idu[:, j, :], axis=0),
                    yout[:, j % 2, :], None, compute_op=ALU.add).then_inc(added, 16)

            tiles(add_rows)(pool)
            pool.wait_ge(added, 16 * NT)

        @block.scalar
        def _(act):
            act.dma_start(W[:, :, :], t["W"]).then_inc(W_in, 16)
            for dst, src in ((gw, "gate_w"), (b1, "b1")):
                act.dma_start(dst[:, :, :], t[src]).then_inc(small_in, 16)
            for dst, src in ((gb, "gate_b"), (gnnb, "gnn_b")):
                act.dma_start(dst[:, :], t[src]).then_inc(small_in, 16)

            def copy_xnT(n):
                act.wait_ge(xnT_psum, n + 1)
                if n >= 2:
                    if n - 2 < T:
                        act.wait_ge(Y_psum, n - 1)
                    else:
                        act.wait_ge(logits_psum, n - T - 1)
                act.activation(xnT[:, n % 2, :], turned(n % 2), ACT.Copy).then_inc(xnT_ready, 1)

            def copy_Y(i):
                act.wait_ge(Y_psum, i + 1)
                act.wait_ge(dinv_ready, i + 1)
                act.activation(Y[:, i, :], psum_Y(i % 2), ACT.Copy, scale=dinv[:, i:i + 1])\
                   .then_inc(Y_ready, 1)

            def normalise_x(i):
                act.wait_ge(nmr_ready, i // (T // XG) + 1)
                if i >= 2:
                    act.wait_ge(xnT_psum, i - 1)
                act.activation(xn[:, i % 2, :], x_all[:, i, :], ACT.Identity,
                               bias=nmr[:, i:i + 1], scale=rstd[:, i:i + 1]).then_inc(xn_ready, 1)

            normalise_x(0)
            for i in range(T + 2):
                if i + 1 < T:
                    normalise_x(i + 1)
                if i < T:
                    copy_xnT(i)
                if i >= 2:
                    copy_Y(i - 2)

            def square_sum(n, q):
                act.wait_ge(w_in[n % 2][q], 16 * (n // 2 + 1))
                if n or q:
                    act.wait_ge(squares, 3 * n + q)
                act.activation(junk, stage[:, (n + 1) % 2, q, :], ACT.Square,
                               accum_out=ss[:, n, q:q + 1]).then_inc(squares, 1)
                if q == 1:
                    act.wait_ge(squares, 3 * n + 2)
                    act.activation(junk[:, 0:HT], b1[:, PREP[n], :], ACT.Square,
                                   accum_out=ss[:, n, 2:3]).then_inc(squares, 1)

            def hi_part(n, q):
                e = PREP[n]
                w2 = w2v[:, e, :].rearrange("p (h q d) -> p h q d", q=2, d=D)
                outs = w1v[:, e, 0:WCOLS], w2[:, :, 0, :]
                src = (stage[:, (n + 1) % 2, 0, :],
                       stage[:, (n + 1) % 2, 1, :].rearrange("p (h d) -> p h d", d=D))
                act.wait_ge(scale_ready, n + 1)
                act.wait_ge(agg_ready, min(2 * n + 2 + q, T))
                act.activation(outs[q], src[q], ACT.Copy,
                               scale=sc[:, e, q:q + 1].bitcast(F32)).then_inc(hi_ready, 1)

            act.wait_ge(small_in, 16 * 4)
            square_sum(0, 0)
            for s in range(T + 1):
                if s >= 1:
                    b = (s - 1) % 2
                    act.wait_ge(negm_ready, s)
                    act.activation(ex[:, b, :], lg[:, b, :], ACT.Exp, bias=negm[:, b, :],
                                   accum_out=sumex[:, b, :]).then_inc(exp_ready, 1)
                if s < T:
                    act.wait_ge(xn_ready, T + s + 1)
                    if s >= RB:
                        act.wait_ge(scattered[s % RB], 16 * TOPK * (s // RB))
                    act.activation(row[:, s % RB, 0:D].bitcast(F16)[:, 0:D], xn[:, s % 2, :],
                                   ACT.Copy, scale=XSCALE).then_inc(row_hi, 1)
                    copy_xnT(T + s)
                if 1 <= s < T - 1:
                    hi_part((s - 1) // 2, (s - 1) % 2)
                if s + 1 < T:
                    square_sum((s + 1) // 2, (s + 1) % 2)
            hi_part(E - 1, 0)
            pad_regions(act, mybir.EngineType.Activation, range(1, E, 2))
            hi_part(E - 1, 1)
            act.activation(warm[:, :], onesf[:, 0:1], ACT.Gelu)

            def copy_xT(u, j):
                act.wait_ge(xT_psum, u * U + j + 1)
                act.sem_inc(act_step, 1)
                if not (isinstance(u, int) and u * U + j < 2):
                    act.wait_ge(h_psum, HT // 2 * (u * U + j - 1))
                    act.sem_inc(act_step, 1)
                act.activation(xT[:, j % 2, :], PS[:, 6 + j % 2, 0:D].bitcast(F16), ACT.Copy)\
                   .then_inc(xT_ready, 1)

            def gelus(u, j, rows=None):
                tau = u * U + j
                e = act.value_load(etab[0:1, bass.ds(tau, 1)], min_val=0, max_val=E - 1)
                for h in range(HT):
                    if h % 2 == 0:
                        act.wait_ge(h_psum, HT // 2 * tau + h // 2 + 1)
                        act.sem_inc(act_step, 1)
                    if h == 0 and not (isinstance(u, int) and tau < 2):
                        act.wait_ge(h_split, 2 * tau - 2)
                        act.sem_inc(act_step, 1)
                    act.activation(
                        g[:, j % 2, h * P:(h + 1) * P],
                        psum_h(h), ACT.Gelu,
                        bias=b1[:, bass.ds(e, 1), h:h + 1].rearrange("p a b -> p (a b)"),
                        scale=inv1[:, bass.ds(e, 1)]).then_inc(g_ready, 1)
                    if h == HT // 2 + 1 and rows:
                        copy_xT(*rows)

            act.wait_ge(tables, 1)
            copy_xT(0, 0)
            copy_xT(0, 1)
            gelus(0, 0)

            def body(u, j):
                if nxt := later(u, j, 1):
                    gelus(*nxt, rows=later(u, j, 2))

            tiles(body)(act)

        @block.vector
        def _(dve):
            n = [0]

            def mark(ins):
                n[0] += 1
                ins.then_inc(dve_chain, 1)
                return n[0]

            def link(ins):
                dve.wait_ge(dve_chain, mark(ins))

            G = T // XG

            def statistics(g):
                dve.wait_ge(x_in[g], 16)
                for i in range(g * G, (g + 1) * G):
                    last = dve.bn_stats(stats[:, i, :], x_all[:, i, :])
                link(last)
                for i in range(g * G, (g + 1) * G):
                    last = dve.bn_aggr(mv[:, i, :], stats[:, i, :])
                link(last)
                dve.tensor_scalar(veps[:, g * G:(g + 1) * G], mv[:, g * G:(g + 1) * G, 1], EPS,
                                  None, ALU.add).then_inc(veps_ready, 1)

            def shift(g):
                part = slice(g * G, (g + 1) * G)
                dve.wait_ge(rstd_ready, g + 1)
                dve.scalar_tensor_tensor(nmr[:, part], mv[:, part, 0], -1.0, rstd[:, part],
                                         ALU.mult, ALU.mult).then_inc(nmr_ready, 1)

            def degree(i):
                dve.wait_ge(rowsum_ready, i + 1)
                dve.tensor_copy(deg[:, i:i + 1], psum_sum(i))
                dve.tensor_scalar(dmax[:, i:i + 1], psum_sum(i), 2.0 ** -126, None,
                                  ALU.max).then_inc(deg_ready, 1)

            def inverse_root(i):
                dve.wait_ge(deg_pow, i + 1)
                dve.scalar_tensor_tensor(dinv[:, i:i + 1], deg[:, i:i + 1], 0.0,
                                         dpow[:, i:i + 1], ALU.is_gt, ALU.mult)\
                   .then_inc(dinv_ready, 1)

            statistics(0)
            shift(0)
            for i in range(T + 2):
                if i < T:
                    dve.wait_ge(adj_in[i], 16)
                    if i >= 2:
                        dve.wait_ge(rowsum_ready, i - 1)
                    dve.tensor_reduce(
                        red[:, i % 2, :],
                        arena[:, i * N:(i + 1) * N].rearrange("p (k c) -> p c k", k=T),
                        AX.X, ALU.add).then_inc(red_ready, 1)
                if i % 2 == 0 and 1 <= i // 2 < XG:
                    statistics(i // 2)
                if 1 <= i <= T:
                    degree(i - 1)
                if i % 2 and 1 <= i // 2 < XG:
                    shift(i // 2)
                if i >= 2:
                    inverse_root(i - 2)

            dve.wait_ge(small_in, 16 * 4)

            def linear(s):
                i = ORDER[s]
                dve.wait_ge(agg_ready, s + 1)
                if s == 0:
                    dve.wait_ge(dinv_ready, T)
                dve.scalar_tensor_tensor(lin, region(s), dinv[:, i:i + 1], gnnb[:, :],
                                         ALU.mult, ALU.add).then_inc(lin_done, 1)

            def add_x(s):
                b = s % 2
                dve.wait_ge(lin_done, s + 1)
                dve.wait_ge(again_in[b], 16 * (s // 2 + 1))
                dve.scalar_tensor_tensor(x1[:, b, :], lin, 0.0, x1[:, b, :],
                                         ALU.max, ALU.add).then_inc(x1_ready, 1)

            def moments(s):
                dve.wait_ge(x1_ready, s + 1)
                return mark(dve.bn_stats(stats2[:, s % 2, :], x1[:, s % 2, :]))

            def variance(s, moments_):
                dve.wait_ge(dve_chain, moments_)
                return mark(dve.bn_aggr(mv2[:, s % 2, :], stats2[:, s % 2, :]))

            def add_eps(s, variance_):
                dve.wait_ge(dve_chain, variance_)
                dve.tensor_scalar(veps2[:, s % 2, :], mv2[:, s % 2, 1:2], EPS, None, ALU.add)\
                   .then_inc(veps2_ready, 1)

            def normalise(s):
                b = s % 2
                dve.wait_ge(rstd2_ready, s + 1)
                dve.wait_ge(xnT_psum, T + s - 1)
                if s >= 2:
                    dve.wait_ge(row_hi, s - 1)
                dve.tensor_scalar(xn[:, b, :], x1[:, b, :], mv2[:, b, 0:1], rstd2[:, b, :],
                                  ALU.subtract, ALU.mult).then_inc(xn_ready, 1)

            def row_rest(s):
                words = row[:, s % RB, 0:D].bitcast(F16)
                dve.wait_ge(row_hi, s + 1)
                dve.tensor_copy(row[:, s % RB, IDCOL:IDCOL + 1], tokid[:, ORDER[s]:ORDER[s] + 1])
                dve.scalar_tensor_tensor(words[:, D:2 * D], xn[:, s % 2, :], XSCALE,
                                         words[:, 0:D], ALU.mult, ALU.subtract)

            def read_logits(s):
                dve.wait_ge(logits_psum, s + 1)
                dve.tensor_tensor(lg[:, s % 2, :], psum_logits, gb[:, :], ALU.add)\
                   .then_inc(logits_read, 1)

            def sort(s):
                dve.wait_ge(logits_read, s + 1)
                return mark(dve.max(top8[:, s % 2, :], lg[:, s % 2, :]))

            def find(s, sorted_):
                b = s % 2
                dve.wait_ge(dve_chain, sorted_)
                dve.tensor_scalar(negm[:, b, :], top8[:, b, 0:1], -1.0, None, ALU.mult)\
                   .then_inc(negm_ready, 1)
                return mark(dve.max_index(idx8[:, :], top8[:, b, :], lg[:, b, :]))

            def to_float(found):
                dve.wait_ge(dve_chain, found)
                return mark(dve.tensor_copy(idxf[:, :], idx8[:, 0:TOPK]))

            def one_hot(s, indices):
                dve.wait_ge(dve_chain, indices)
                for k in range(TOPK):
                    last = dve.tensor_scalar(oh[:, s % 2, k, :], iota8[:, :], idxf[:, k:k + 1],
                                             None, ALU.is_equal)
                return mark(last)

            def chosen(s, one_hot_):
                b = s % 2
                dve.wait_ge(dve_chain, one_hot_)
                return mark(dve.tensor_tensor(mask[:, b, :], oh[:, b, 0, :], oh[:, b, 1, :],
                                              ALU.add))

            def accumulate(s, chosen_):
                dve.wait_ge(dve_chain, chosen_)
                dve.tensor_tensor(cum[:, s + 1, :], cum[:, s, :], mask[:, s % 2, :], ALU.add)\
                   .then_inc(cum_ready, 1)

            def inverse_sum(s):
                dve.wait_ge(exp_ready, s + 1)
                return mark(dve.reciprocal(rsum[:, s % 2, :], sumex[:, s % 2, :]))

            def gates(s, inverse):
                b = s % 2
                dve.wait_ge(dve_chain, inverse)
                dve.scalar_tensor_tensor(row[:, s % RB, GATE0:GATE0 + E], ex[:, b, :],
                                         rsum[:, b, :], mask[:, b, :], ALU.mult, ALU.mult)

            def read_ranks(s):
                dve.wait_ge(rank_psum, s + 1)
                dve.tensor_tensor(base[:, :], psum_rank(s), eoff[:, :], ALU.add)\
                   .then_inc(rank_read, 1)

            def own_ranks(s):
                dve.wait_ge(rank_read, s + 1)
                for k in range(TOPK):
                    last = dve.tensor_tensor_reduce(tmp8[:, k, :], oh[:, s % 2, k, :], base[:, :],
                                                    1.0, 0.0, ALU.mult, ALU.add, slotf[:, k:k + 1])
                return mark(last)

            def slots(s, ranks_):
                dve.wait_ge(dve_chain, ranks_)
                dve.tensor_copy(slot[:, s % RB, :], slotf[:, :]).then_inc(slot_ready, 1)

            def bias_share(n):
                dve.wait_ge(norm_psum, n + 1)
                return mark(dve.tensor_scalar(ntmp[:, :], psum_norm[:, 2:3], 2.0, None, ALU.mult))

            def bounds(n, share):
                dve.tensor_copy(nsum[:, 0:2], psum_norm[:, 0:2])
                dve.wait_ge(dve_chain, share)
                dve.scalar_tensor_tensor(nsum[:, 2:3], psum_norm[:, 0:1], 2.0 * D, ntmp[:, :],
                                         ALU.mult, ALU.add).then_inc(norm_sum, 1)

            def exponents(n):
                dve.wait_ge(norm_sum, n + 1)
                return mark(dve.tensor_scalar(mexp[:, :], nsum[:, :].bitcast(I32), 24, None,
                                              ALU.logical_shift_right))

            def powers(n, exponents_):
                dve.wait_ge(dve_chain, exponents_)
                dve.tensor_scalar(sc[:, PREP[n], :], mexp[:, :], -float(EXPO_UNIT),
                                  204.0 * EXPO_UNIT, ALU.mult, ALU.add).then_inc(scale_ready, 1)
                return mark(dve.tensor_scalar(inv[:, :], mexp[:, :], float(EXPO_UNIT),
                                              50.0 * EXPO_UNIT, ALU.mult, ALU.add))

            def inverses(n, powers_):
                e, invf = PREP[n], inv[:, :].bitcast(F32)
                dve.wait_ge(dve_chain, powers_)
                dve.tensor_scalar(inv1[:, e:e + 1], invf[:, 0:1], 1.0 / XSCALE, None, ALU.mult)
                dve.tensor_tensor(inv2[:, e:e + 1], invf[:, 1:2], invf[:, 2:3], ALU.mult)

            def lo_part(n, q):
                e = PREP[n]
                w2 = w2v[:, e, :].rearrange("p (h q d) -> p h q d", q=2, d=D)
                outs = w1v[:, e, WCOLS:2 * WCOLS], w2[:, :, 1, :]
                his = w1v[:, e, 0:WCOLS], w2[:, :, 0, :]
                src = (stage[:, (n + 1) % 2, 0, :],
                       stage[:, (n + 1) % 2, 1, :].rearrange("p (h d) -> p h d", d=D))
                dve.wait_ge(hi_ready, 2 * n + q + 1)
                dve.scalar_tensor_tensor(outs[q], src[q], sc[:, e, q:q + 1].bitcast(F32),
                                         his[q], ALU.mult, ALU.subtract).then_inc(lo_ready, 1)

            for s in range(T):
                r, c = s >= 2, s >= 1
                if r:
                    read_ranks(s - 2)
                linear(s)
                if r:
                    m_rank = own_ranks(s - 2)
                if c:
                    read_logits(s - 1)
                add_x(s)
                if c:
                    m_sort = sort(s - 1)
                if r:
                    slots(s - 2, m_rank)
                m_moments = moments(s)
                if c:
                    m_find = find(s - 1, m_sort)
                m_variance = variance(s, m_moments)
                if c:
                    m_float = to_float(m_find)
                add_eps(s, m_variance)
                if c:
                    m_hot = one_hot(s - 1, m_float)
                    m_chosen = chosen(s - 1, m_hot)
                    m_inverse = inverse_sum(s - 1)
                    accumulate(s - 1, m_chosen)
                normalise(s)
                if s % 2:
                    m_share = bias_share(s // 2)
                if c:
                    gates(s - 1, m_inverse)
                if s % 2:
                    bounds(s // 2, m_share)
                    m_expo = exponents(s // 2)
                    m_powers = powers(s // 2, m_expo)
                if r and s < T - 1:
                    lo_part((s - 2) // 2, s % 2)
                row_rest(s)
                if s % 2:
                    inverses(s // 2, m_powers)
            read_ranks(T - 2)
            m_rank = own_ranks(T - 2)
            slots(T - 2, m_rank)
            read_logits(T - 1)
            m_find = find(T - 1, sort(T - 1))
            m_hot = one_hot(T - 1, to_float(m_find))
            accumulate(T - 1, chosen(T - 1, m_hot))
            gates(T - 1, inverse_sum(T - 1))
            read_ranks(T - 1)
            slots(T - 1, own_ranks(T - 1))

            dve.wait_ge(count_psum, 1)
            dve.tensor_tensor(ptab[0:1, :], psum_count[0:1, :], eoff[0:1, :], ALU.add)\
               .then_inc(ptab_ready, 1)
            link(dve.tensor_scalar(tli[:, 0, :], psum_count, float(P - 1), None, ALU.add))
            link(dve.tensor_scalar(tli[:, 1, :], tli[:, 0, :], P.bit_length() - 1, None,
                                   ALU.logical_shift_right))
            link(dve.tensor_copy(tl[:, 0, :], tli[:, 1, :]))
            link(dve.tensor_tensor_scan(tl[:, 1, :], onesf[:, 0:E], tl[:, 0, :], 0.0,
                                        ALU.mult, ALU.add))
            def over_tiles(v):
                return v.unsqueeze(2).to_broadcast([1, E, NTX])

            link(dve.tensor_tensor(cmp[:, 0, :, :],
                                   iotat[0:1, :].unsqueeze(1).to_broadcast([1, E, NTX]),
                                   over_tiles(tl[0:1, 1, :]), ALU.is_ge))
            link(dve.tensor_tensor(cmp[:, 1, :, :], cmp[:, 0, :, :], over_tiles(tl[0:1, 0, :]),
                                   ALU.mult))
            for q in range(2):
                last = dve.tensor_reduce(tt[:, q, :], cmp[:, q, :, :].rearrange("p e t -> p t e"),
                                         AX.X, ALU.add)
            link(last)
            link(dve.tensor_tensor(tt[:, 2, :], iotat[0:1, :], tt[:, 1, :], ALU.subtract))
            link(dve.tensor_scalar(tt[:, 3, :], tt[:, 2, :], float(P), None, ALU.mult))
            link(dve.scalar_tensor_tensor(tt[:, 4, :], tt[:, 0, :], float(REGION), tt[:, 3, :],
                                          ALU.mult, ALU.add))
            dve.tensor_scalar(rtab[:, :], tt[:, 4, :], float(EMPTY), None, ALU.min)\
               .then_inc(rows_known, 1)
            link(dve.tensor_scalar(tt[:, 1, :], tt[:, 0, :], float(E - 1), None, ALU.min))
            dve.tensor_copy(etab[:, :], tt[:, 1, :])

            def every(i):
                return tt[:, 1, i:i + PACK * (WORDS - 1) + 1:PACK]

            def join(o, high, i, low):
                return dve.scalar_tensor_tensor(o, high, float(1 << BITS * i), low, ALU.mult,
                                                ALU.add)

            join(pk[:, 0, :], every(1), 1, every(0))
            link(join(pk[:, 1, :], every(3), 1, every(2)))
            link(join(pk[:, 2, :], pk[:, 1, :], 2, pk[:, 0, :]))
            join(packed[:, :], every(4), PACK, pk[:, 2, :]).then_inc(tables, 1)

            lo_part(E - 2, 1)
            for q in range(2):
                lo_part(E - 1, q)

            dve.wait_ge(tables, 1)

            def expert(u, j):
                return dve.value_load(etab[0:1, bass.ds(u * U + j, 1)], min_val=0, max_val=E - 1)

            def split(e, u, j, q):
                tau = u * U + j
                s = sc[:, :, :].bitcast(F32)[:, bass.ds(e, 1), 2:3].rearrange("p a b -> p (a b)")
                half = H // 2
                cols = slice(q * half, (q + 1) * half)
                dve.wait_ge(g_ready, HT * tau + (q + 1) * HT // 2)
                dve.sem_inc(dve_step, 1)
                if q == 0 and not (isinstance(u, int) and tau < 2):
                    dve.wait_ge(y_psum, tau - 1)
                    dve.sem_inc(dve_step, 1)
                dve.tensor_scalar(hs[:, j % 2, 0, cols], g[:, j % 2, cols], s, None,
                                  ALU.mult).then_inc(h_hi, 1)
                dve.wait_ge(h_hi, 2 * tau + q + 1)
                dve.sem_inc(dve_step, 1)
                dve.scalar_tensor_tensor(hs[:, j % 2, 1, cols], g[:, j % 2, cols], s,
                                         hs[:, j % 2, 0, cols], ALU.mult, ALU.subtract)\
                   .then_inc(h_split, 1)

            def slot_values(e, u, j):
                gate = xrow[:, j, GATE0:GATE0 + E][:, bass.ds(e, 1)]
                dve.wait_ge(xrow_in[j], (u + 1) * 16)
                dve.sem_inc(dve_step, 1)
                if not (isinstance(u, int) and u == 0):
                    dve.wait_ge(added, (u * U + j - U + 1) * 16)
                    dve.sem_inc(dve_step, 1)
                dve.tensor_copy(idu[:, j, :], xrow[:, j, IDCOL:IDCOL + 1])
                dve.tensor_tensor(gs[:, j % 2, :], gate, inv2[:, bass.ds(e, 1)], ALU.mult)
                dve.tensor_scalar(yb[:, j % 2, :],
                                  b2r[:, bass.ds(e, 1), :].rearrange("p a b -> p (a b)"),
                                  gate, None, ALU.mult).then_inc(yb_ready, 1)

            def add_up(u, j):
                tau = u * U + j
                o, p = yout[:, j % 2, :], PS[:, 4 + j % 2, :]
                if not (isinstance(u, int) and tau < 2):
                    dve.wait_ge(added, (tau - 1) * 16)
                    dve.sem_inc(dve_step, 1)
                dve.wait_ge(yb_ready, tau + 1)
                dve.sem_inc(dve_step, 1)
                dve.wait_ge(y_psum, tau + 1)
                dve.sem_inc(dve_step, 1)
                dve.scalar_tensor_tensor(o, p[:, 0:D], gs[:, j % 2, :], yb[:, j % 2, :],
                                         ALU.mult, ALU.add).then_inc(y_half, 1)
                dve.wait_ge(y_half, tau + 1)
                dve.sem_inc(dve_step, 1)
                dve.scalar_tensor_tensor(o, p[:, D:2 * D], gs[:, j % 2, :], o,
                                         ALU.mult, ALU.add).then_inc(y_ready, 1)

            dve.wait_ge(late_in, 16)
            e0 = expert(0, 0)
            split(e0, 0, 0, 0)
            slot_values(e0, 0, 0)
            split(e0, 0, 0, 1)

            def body(u, j):
                nxt = later(u, j, 1)
                if nxt:
                    e = expert(*nxt)
                    split(e, *nxt, 0)
                    slot_values(e, *nxt)
                    split(e, *nxt, 1)
                add_up(u, j)

            tiles(body)(dve)

        @block.tensor
        def _(pe):
            def transposes(n):
                pe.wait_ge(xn_ready, n + 1)
                if n >= 2:
                    pe.wait_ge(xnT_ready, n - 1)
                if n >= T + 2:
                    pe.wait_ge(rank_read, n - T - 1)
                for k in range(KD):
                    last = pe.transpose(turned(n % 2)[:, k * P:(k + 1) * P],
                                        xn[:, n % 2, k * P:(k + 1) * P], identf[:, :])
                last.then_inc(xnT_psum, 1)

            def product_W(i):
                pe.wait_ge(xnT_ready, i + 1)
                if i >= 2:
                    pe.wait_ge(Y_ready, i - 1)
                for k in range(KD):
                    last = pe.matmul(psum_Y(i % 2), xnT[:, i % 2, k * P:(k + 1) * P],
                                     W[:, k, :], start=(k == 0), stop=(k == KD - 1))
                last.then_inc(Y_psum, 1)

            def rowsum(i):
                pe.wait_ge(red_ready, i + 1)
                if i:
                    pe.wait_ge(deg_ready, i)
                pe.matmul(psum_sum(i), red[:, i % 2, :], onesf[:, 0:1], start=True,
                          stop=True).then_inc(rowsum_ready, 1)

            def adj_product(s, ks, first=False):
                i, r = ORDER[s], region(s)
                before_it = [p for p in range(s) if BANKS[p] == BANKS[s]]
                if before_it and not first:
                    pe.wait_ge(lin_done, before_it[-1] + 1)
                for k in ks:
                    if s == 0 or first:
                        pe.wait_ge(Y_ready, k + 1)
                    c = i * N + k * P
                    last = pe.matmul(r, arena[:, c:c + P], Y[:, k, :],
                                     start=(k == 0 and not (i < EARLY and i % 2)),
                                     stop=(k == T - 1), skip_group_check=True)
                if ks[-1] == T - 1:
                    last.then_inc(agg_ready, 1)

            def logits(s):
                pe.wait_ge(xnT_ready, T + s + 1)
                if s:
                    pe.wait_ge(logits_read, s)
                    pe.wait_ge(norm_sum, (s + 1) // 2)
                for k in range(KD):
                    last = pe.matmul(psum_logits, xnT[:, s % 2, k * P:(k + 1) * P], gw[:, k, :],
                                     start=(k == 0), stop=(k == KD - 1))
                last.then_inc(logits_psum, 1)

            def ranks(s):
                pe.wait_ge(cum_ready, s + 1)
                pe.matmul(psum_rank(s), before[:, :], mask[:, s % 2, :], start=True, stop=False)
                pe.matmul(psum_rank(s), onesb[:, :], cum[:, s, :], start=False, stop=True)\
                  .then_inc(rank_psum, 1)

            def norms(n):
                pe.wait_ge(squares, 3 * n + 3)
                pe.wait_ge(logits_read, 2 * n + 1)
                pe.matmul(psum_norm, onesf[:, :], ss[:, n, :], start=True, stop=True)\
                  .then_inc(norm_psum, 1)

            pe.wait_ge(consts, 1)
            pe.wait_ge(W_in, 16)
            early = [(ORDER.index(i), k) for ks in EARLY_ROUNDS for i in range(EARLY) for k in ks]
            for i in range(T + 1):
                if i < T:
                    transposes(i)
                if i:
                    product_W(i - 1)
                if i < T:
                    rowsum(i)
                for _ in range(0 if i < 4 else 2 if i <= 8 else 4):
                    at, k = early.pop(0)
                    adj_product(at, (k,), first=True)

            pe.wait_ge(small_in, 16 * 4)
            for s in range(T + 1):
                if s < T:
                    done = EARLY_KS if ORDER[s] < EARLY else 0
                    cuts = [done, max(9, done + 2), T - 5, T]
                    adj_product(s, range(cuts[0], cuts[1]))
                if s % 2 == 0 and s >= 2:
                    norms(s // 2 - 1)
                if s < T:
                    adj_product(s, range(cuts[1], cuts[2]))
                if 1 <= s <= T:
                    transposes(T + s - 1)
                if s >= 2:
                    ranks(s - 2)
                if s < T:
                    adj_product(s, range(cuts[2], T))
                if s >= 1:
                    logits(s - 1)
            ranks(T - 1)
            pe.wait_ge(logits_read, T)
            pe.matmul(psum_count, onesb[:, :], cum[:, T, :], start=True, stop=True)\
              .then_inc(count_psum, 1)

            pe.wait_ge(rank_read, T)

            def experts(u):
                _, words = nc.values_load_multi_w_load_instructions(
                    packed[0:1, bass.ds(2 * u, 2)], engines=[mybir.EngineType.PE], min_val=0,
                    max_val=(1 << BITS * (PACK + 1)) - 1)
                mask_ = (1 << BITS) - 1
                return [(w >> BITS * i) & mask_ for w in words for i in range(PACK)] + \
                    [(words[1] >> BITS * PACK) & mask_]

            def w1_at(e, q, c):
                c += q * WCOLS
                return w1v[:, bass.ds(e, 1), c:c + P].rearrange("p a b -> p (a b)")

            def w2_at(e, h):
                return w2v[:, bass.ds(e, 1), 2 * h * D:2 * (h + 1) * D]\
                    .rearrange("p a b -> p (a b)")

            def turn_rows(u, j):
                pe.wait_ge(xrow_in[j], (u + 1) * 16)
                words = xrow[:, j, 0:D].bitcast(F16)
                for k in range(2 * KD):
                    last = pe.transpose(PS[:, 6 + j % 2, 0:D].bitcast(F16)[:, k * P:(k + 1) * P],
                                        words[:, k * P:(k + 1) * P], identh[:, :])
                last.then_inc(xT_psum, 1)

            def up(e, u, j, h):
                if h == 0:
                    pe.wait_ge(xT_ready, u * U + j + 1)
                o = psum_h(h)
                for k in range(KD):
                    c = k * H + h * P
                    x_hi = xT[:, j % 2, k * P:(k + 1) * P]
                    x_lo = xT[:, j % 2, (KD + k) * P:(KD + k + 1) * P]
                    hi = w1_at(e, 0, c)
                    pe.matmul(o, hi, x_hi, start=(k == 0), stop=False)
                    pe.matmul(o, hi, x_lo, start=False, stop=False)
                    last = pe.matmul(o, w1_at(e, 1, c), x_hi, start=False, stop=(k == KD - 1))
                if h % 2:
                    last.then_inc(h_psum, 1)

            def down(e, u, j, h):
                if h % (HT // 2) == 0:
                    pe.wait_ge(h_split, 2 * (u * U + j) + h // (HT // 2) + 1)
                o, w = PS[:, 4 + j % 2, :], w2_at(e, h)
                cols = slice(h * P, (h + 1) * P)
                pe.matmul(o, hs[:, j % 2, 0, cols], w, start=(h == 0), stop=False)
                last = pe.matmul(o[:, 0:D], hs[:, j % 2, 1, cols], w[:, 0:D], start=False,
                                 stop=(h == HT - 1))
                if h == HT - 1:
                    last.then_inc(y_psum, 1)

            pe.wait_ge(tables, 1)
            first = experts(0)
            turn_rows(0, 0)
            turn_rows(0, 1)
            pe.wait_ge(lo_ready, 2 * E)
            for h in range(HT):
                up(first[0], 0, 0, h)
            known = {}

            def body(u, j):
                if j == 0:
                    known[0] = first if isinstance(u, int) and u == 0 else experts(u)
                e = known[0]
                nxt, after = later(u, j, 1), later(u, j, 2)
                for h in range(HT):
                    down(e[j], u, j, h)
                    if nxt:
                        up(e[j + 1], *nxt, h)
                    if h == HT // 2 - 1 and after:
                        turn_rows(*after)

            tiles(body)(pe)


def kernel(**inputs):
    import numpy as np
    import concourse.bacc as bacc
    from concourse.bass_utils import run_bass_kernel_spmd

    def rows(a, p=P):
        return np.broadcast_to(np.asarray(a).reshape(1, -1), (p, np.asarray(a).size))

    i = {k: np.asarray(v) for k, v in inputs.items()}
    arrays = {
        "x": i["x"].reshape(T, P, D).transpose(1, 0, 2),
        "adjT": i["adj"].reshape(T, P, T, P).transpose(0, 3, 2, 1).reshape(T, P, N),
        "W": i["L0_gnn_W"].reshape(KD, P, D).transpose(1, 0, 2),
        "gnn_b": rows(i["L0_gnn_b"]),
        "gate_w": i["L0_ffn_gate_w"].reshape(KD, P, E).transpose(1, 0, 2),
        "gate_b": rows(i["L0_ffn_gate_b"]),
        "w1": i["L0_ffn_w1"].reshape(E, KD, P, H).transpose(0, 2, 1, 3).reshape(E, P, WCOLS),
        "b1": i["L0_ffn_b1"].reshape(E, HT, P).transpose(2, 0, 1),
        "w2": i["L0_ffn_w2"].reshape(E, HT, P, D).transpose(0, 2, 1, 3).reshape(E, P, WCOLS),
        "b2": rows(i["L0_ffn_b2"]).reshape(P, E, D),
    }
    arrays = {f"{k}_in": np.ascontiguousarray(v) for k, v in arrays.items()}
    nc = bacc.Bacc("TRN2", target_bir_lowering=False, num_devices=1)
    t = {k[:-3]: nc.dram_tensor(k, v.shape, F32, kind="ExternalInput").ap()
         for k, v in arrays.items()}
    t["out"] = nc.dram_tensor("y_out", (N + P, D), F32, kind="ExternalOutput").ap()
    build(nc, t)
    r = run_bass_kernel_spmd(nc, [arrays], core_ids=[0])
    return r.results[0]["y_out"][:N]
```
